# Optimizing a Trainium2 kernel written in Bass

```python
import numpy as np
import jax
import jax.numpy as jnp

def _softmax(x, axis=-1):
    return jax.nn.softmax(x, axis=axis)

def _gelu(x):
    return jax.nn.gelu(x, approximate=True)

def _silu(x):
    return jax.nn.silu(x)

def _sigmoid(x):
    return jax.nn.sigmoid(x)

def _layernorm(x, axis=-1, eps=1e-05):
    m = jnp.mean(x, axis=axis, keepdims=True)
    v = jnp.var(x, axis=axis, keepdims=True)
    return (x - m) / jnp.sqrt(v + eps)

def _scatter_add(tgt, idx, src, axis=0):
    return tgt.at[idx].add(src)

def _segment_sum(src, seg, n):
    return jax.ops.segment_sum(src, seg, n)
kernel_name = 'mk_seq_postln_d1_jaxref_r8_68060a'

def setup_inputs(seed: int=0):
    np.random.seed(seed)
    _w = jnp.asarray

    def _L0_attn_setup():
        import math
        import jax, jax.numpy as jnp
        import numpy as np
        D, DK, DV = (128, 128, 128)
        B, S = (4, 256)
        key = jax.random.key(seed)
        ks = jax.random.split(key, 4)
        std_qk = math.sqrt(2.0 / (D + DK))
        std_v = math.sqrt(2.0 / (D + DV))
        return {'X': jax.random.normal(ks[0], (B, S, D), dtype=jnp.float32), 'W_q': jax.random.normal(ks[1], (D, DK), dtype=jnp.float32) * std_qk, 'W_k': jax.random.normal(ks[2], (D, DK), dtype=jnp.float32) * std_qk, 'W_v': jax.random.normal(ks[3], (D, DV), dtype=jnp.float32) * std_v, 'b_q': jnp.zeros((DK,), dtype=jnp.float32), 'b_k': jnp.zeros((DK,), dtype=jnp.float32), 'b_v': jnp.zeros((DV,), dtype=jnp.float32)}
    _L0_attn_in = _L0_attn_setup()

    def _L0_ffn_setup():
        import jax, jax.numpy as jnp
        import numpy as np
        D_IN, D_HID = (128, 512)

        def _ternary(key, shape):
            return jax.random.randint(key, shape, -1, 2).astype(jnp.float32)

        def _tlin(x, w, s):
            return jnp.einsum('bsi,oi->bso', x, w) * s
        key = jax.random.key(seed)
        ks = jax.random.split(key, 12)
        inv = lambda fan: 1.0 / np.sqrt(fan).astype(np.float32)
        return {'x': jax.random.normal(ks[0], (4, 256, D_IN), dtype=jnp.float32), 'w1_w': _ternary(ks[1], (D_HID, D_IN)), 'w1_s': jax.random.uniform(ks[2], (D_HID,), dtype=jnp.float32) * inv(D_IN), 'w2_w': _ternary(ks[3], (D_HID, D_IN)), 'w2_s': jax.random.uniform(ks[4], (D_HID,), dtype=jnp.float32) * inv(D_IN), 'h1_w': _ternary(ks[5], (D_HID, D_HID)), 'h1_s': jax.random.uniform(ks[6], (D_HID,), dtype=jnp.float32) * inv(D_HID), 'h2_w': _ternary(ks[7], (D_HID, D_HID)), 'h2_s': jax.random.uniform(ks[8], (D_HID,), dtype=jnp.float32) * inv(D_HID), 'w3_w': _ternary(ks[9], (D_IN, D_HID)), 'w3_s': jax.random.uniform(ks[10], (D_IN,), dtype=jnp.float32) * inv(D_HID)}
    _L0_ffn_in = _L0_ffn_setup()
    _d = {'L0_attn_X': _L0_attn_in['X'], 'L0_attn_W_q': _L0_attn_in['W_q'], 'L0_attn_W_k': _L0_attn_in['W_k'], 'L0_attn_W_v': _L0_attn_in['W_v'], 'L0_attn_b_q': _L0_attn_in['b_q'], 'L0_attn_b_k': _L0_attn_in['b_k'], 'L0_attn_b_v': _L0_attn_in['b_v'], 'L0_ffn_w1_w': _L0_ffn_in['w1_w'], 'L0_ffn_w1_s': _L0_ffn_in['w1_s'], 'L0_ffn_w2_w': _L0_ffn_in['w2_w'], 'L0_ffn_w2_s': _L0_ffn_in['w2_s'], 'L0_ffn_h1_w': _L0_ffn_in['h1_w'], 'L0_ffn_h1_s': _L0_ffn_in['h1_s'], 'L0_ffn_h2_w': _L0_ffn_in['h2_w'], 'L0_ffn_h2_s': _L0_ffn_in['h2_s'], 'L0_ffn_w3_w': _L0_ffn_in['w3_w'], 'L0_ffn_w3_s': _L0_ffn_in['w3_s']}
    _x0 = _d['L0_attn_X']
    _d['L0_attn_X'] = jax.random.normal(jax.random.fold_in(jax.random.key(seed), 1), (2, 1024, 128), dtype=_x0.dtype)
    del _x0
    return _d

def reference(L0_attn_X, L0_attn_W_q, L0_attn_W_k, L0_attn_W_v, L0_attn_b_q, L0_attn_b_k, L0_attn_b_v, L0_ffn_w1_w, L0_ffn_w1_s, L0_ffn_w2_w, L0_ffn_w2_s, L0_ffn_h1_w, L0_ffn_h1_s, L0_ffn_h2_w, L0_ffn_h2_s, L0_ffn_w3_w, L0_ffn_w3_s):

    def _L0_attn_ref(X, W_q, W_k, W_v, b_q, b_k, b_v):
        import math
        import jax, jax.numpy as jnp
        import numpy as np
        D, DK, DV = (128, 128, 128)
        B, S = (4, 256)
        scale = 1.0 / math.sqrt(DK)
        Q = X @ W_q + b_q
        K = X @ W_k + b_k
        V = X @ W_v + b_v
        A = jnp.einsum('bsd,btd->bst', Q, K) * scale
        A = jax.nn.softmax(A, axis=2)
        return jnp.einsum('bst,btv->bsv', A, V)

    def _L0_ffn_ref(x, w1_w, w1_s, w2_w, w2_s, h1_w, h1_s, h2_w, h2_s, w3_w, w3_s):
        import jax, jax.numpy as jnp
        import numpy as np
        D_IN, D_HID = (128, 512)

        def _ternary(key, shape):
            return jax.random.randint(key, shape, -1, 2).astype(jnp.float32)

        def _tlin(x, w, s):
            return jnp.einsum('bsi,oi->bso', x, w) * s
        h = jax.nn.silu(_tlin(x, w1_w, w1_s)) * _tlin(x, w2_w, w2_s)
        h = jax.nn.gelu(_tlin(h, h1_w, h1_s), approximate=False)
        h = jax.nn.gelu(_tlin(h, h2_w, h2_s), approximate=False)
        return _tlin(h, w3_w, w3_s)
    x = L0_attn_X
    x = _layernorm(x + _L0_attn_ref(x, L0_attn_W_q, L0_attn_W_k, L0_attn_W_v, L0_attn_b_q, L0_attn_b_k, L0_attn_b_v), axis=-1)
    x = _layernorm(x + _L0_ffn_ref(x, L0_ffn_w1_w, L0_ffn_w1_s, L0_ffn_w2_w, L0_ffn_w2_s, L0_ffn_h1_w, L0_ffn_h1_s, L0_ffn_h2_w, L0_ffn_h2_s, L0_ffn_w3_w, L0_ffn_w3_s), axis=-1)
    return x

_drawn_inputs = setup_inputs


def setup_inputs(seed=0):
    import zlib

    import numpy as np

    out = dict(_drawn_inputs(seed))
    spreads = {'L0_attn_b_q': (0.0, 0.8), 'L0_attn_b_k': (0.0, 0.8), 'L0_attn_b_v': (0.0, 0.1)}
    factors = {'L0_ffn_w1_w': 8.0,
     'L0_ffn_w1_s': 8.0,
     'L0_ffn_w2_w': 8.0,
     'L0_ffn_w2_s': 8.0,
     'L0_ffn_h1_w': 8.0,
     'L0_ffn_h1_s': 8.0,
     'L0_ffn_h2_w': 8.0,
     'L0_ffn_h2_s': 8.0,
     'L0_ffn_w3_w': 8.0,
     'L0_ffn_w3_s': 8.0}
    for name, (base, spread) in spreads.items():
        noise = np.random.default_rng([zlib.crc32(name.encode()), seed]).standard_normal(out[name].shape)
        drawn = base * np.exp(spread * noise) if base else spread * noise
        out[name] = jnp.asarray(drawn.astype(out[name].dtype))
    for name, factor in factors.items():
        out[name] = (out[name] * factor).astype(out[name].dtype)
    return out
```

```python
from contextlib import ExitStack

import concourse.bass as bass
from concourse import mybir

F32 = mybir.dt.float32
F32R = mybir.dt.float32r
ALU = mybir.AluOpType
ACT = mybir.ActivationFunctionType
AX = mybir.AxisListType

P = 128
B, S, D = 2, 1024, 128
HID = 512
TILE = 512
NT = B * S // TILE
STEPS = B * S // P
PAIRS = STEPS // 2
KB = S // P
HC = HID // P
SCALE = D ** -0.5
EPS = 1e-5

W1, W2, W3, H1, H2 = 0, 1, 2, 3, 3 + HC
WCH = H2 + HC
RAW_SLOTS = 4

BUFS = 2

BQ, BK, S1, S2, HS1, HS2, S3 = 0, 1, 2, 2 + HC, 2 + 2 * HC, 2 + 3 * HC, 2 + 4 * HC
VECS = S3 + 1


def build(nc, xT, x, wqkv, bv, vecs, wffn, eye, out):
    with ExitStack() as ctx:
        def sb(name, shape, dt):
            return ctx.enter_context(nc.sbuf_tensor(name, shape, dt))

        def ps(name, shape):
            return ctx.enter_context(nc.psum_tensor(name, shape, F32))

        def sem(name):
            return ctx.enter_context(nc.semaphore(name))

        arena_a = sb("arena_a", [P, 16384], F32R)
        arena_b = sb("arena_b", [P, 8192], F32R)
        arena_c = sb("arena_c", [P, 6144], F32)
        pt_r = arena_a[:, 0:4096].rearrange("p (a k q) -> p a k q", a=2, k=KB)
        pt_l = arena_a[:, 4096:8192].rearrange("p (a k q) -> p a k q", a=2, k=KB)
        k_r = arena_a[:, 8192:10240]
        k_l = arena_a[:, 10240:12288]
        v_r = arena_a[:, 12288:14336].rearrange("p (n d) -> p n d", d=D)
        v_l = arena_a[:, 14336:16384].rearrange("p (n d) -> p n d", d=D)
        h0_r = arena_a[:, 0:8192].rearrange("p (t c n) -> p t c n", t=NT, c=HC)
        h0_l = arena_a[:, 8192:16384].rearrange("p (t c n) -> p t c n", t=NT, c=HC)
        xt_r = arena_b[:, 0:2048]
        xt_l = arena_b[:, 2048:4096]
        q_r = arena_b[:, 4096:4608].rearrange("p (a q) -> p a q", a=2)
        q_l = arena_b[:, 4608:5120].rearrange("p (a q) -> p a q", a=2)
        w_r = arena_b[:, 5120:5504].rearrange("p (w d) -> p w d", w=3)
        w_l = arena_b[:, 5504:5888].rearrange("p (w d) -> p w d", w=3)
        h1_r = arena_b[:, 0:2048].rearrange("p (c n) -> p c n", c=HC)
        h1_l = arena_b[:, 2048:4096].rearrange("p (c n) -> p c n", c=HC)
        h2_r = arena_b[:, 4096:6144].rearrange("p (c n) -> p c n", c=HC)
        h2_l = arena_b[:, 6144:8192].rearrange("p (c n) -> p c n", c=HC)
        xt32 = arena_c[:, 0:2048]
        q32 = arena_c[:, 2048:4096]
        probs = arena_c[:, 4096:6144].rearrange("p (a k) -> p a k", a=2)
        gate = arena_c[:, 0:1024].rearrange("p (a n) -> p a n", a=2)
        h32 = arena_c[:, 1024:3072].rearrange("p (a n) -> p a n", a=4)
        yT = arena_c[:, 3072:3584]
        z = arena_c[:, 4096:4608].rearrange("p (j d) -> p j d", d=D)

        xn = sb("xn", [P, STEPS, D], F32)
        oT = sb("oT", [P, 2, 256], F32)
        attn = sb("attn", [P, 2, 2, D], F32)
        raw = sb("raw", [P, RAW_SLOTS, 512], F32)
        wf_r = sb("wf_r", [P, WCH, 512], F32R)
        wf_l = sb("wf_l", [P, WCH, 512], F32R)
        w32 = sb("w32", [P, 3, D], F32)
        bvb = sb("bvb", [P, D], F32)
        vec = sb("vec", [P, VECS], F32)
        bqs = sb("bqs", [P, 1], F32)
        ident = sb("ident", [P, P], F32)
        negmax = sb("negmax", [P, STEPS], F32)
        rowsum = sb("rowsum", [P, STEPS], F32)
        rinv = sb("rinv", [P, STEPS], F32)
        bn6 = sb("bn6", [P, 4, 6], F32)
        mv1 = sb("mv1", [P, STEPS, 2], F32)
        rstd1 = sb("rstd1", [P, STEPS], F32)
        mv2 = sb("mv2", [P, 4, 2], F32)
        rstd2 = sb("rstd2", [P, 4], F32)
        low_abs = sb("low_abs", [P, 512], F32)
        low_sum = sb("low_sum", [P, WCH], F32)
        low_flag = sb("low_flag", [1, 1], mybir.dt.int32)
        ones = sb("ones", [P, 1], F32)
        mhalf = sb("mhalf", [P, 4], F32)
        eps = sb("eps", [P, 4], F32)

        psum = ps("psum", [P, 8 * TILE])
        bank = [psum[:, TILE * i:TILE * (i + 1)] for i in range(8)]
        score = [psum[:, 2 * TILE * i:2 * TILE * (i + 1)] for i in range(2)]
        pt_ps = [bank[4], bank[5]]
        pv_ps, misc_ps = bank[6], bank[7]
        gate_ps, up_ps = [bank[0], bank[1]], [bank[2], bank[3]]
        h1_ps, h2_ps = [bank[4], bank[5]], [bank[6], bank[7]]
        y_ps, yn_ps = bank[0], bank[1]

        xT_in = [sem(f"xT_in{t}") for t in range(NT)]
        wqkv_in, small_in, x_in, eye_in, out_stored = (
            sem("wqkv_in"), sem("small_in"), sem("x_in"), sem("eye_in"), sem("out_stored"))
        raw_in = [sem(f"raw_in{n}") for n in range(RAW_SLOTS)]
        wqkv_r, wqkv_l, bqs_ok = sem("wqkv_r"), sem("wqkv_l"), sem("bqs_ok")
        xT_r, xT_l = sem("xT_r"), sem("xT_l")
        k_done, q_done, v_done = sem("k_done"), sem("q_done"), sem("v_done")
        kr_ok, kl_ok, q32_ok = sem("kr_ok"), sem("kl_ok"), sem("q32_ok")
        v32_ok, vr_ok, vl_ok = sem("v32_ok"), sem("vr_ok"), sem("vl_ok")
        qr_ok, ql_ok = sem("qr_ok"), sem("ql_ok")
        s_done, max_ok, exp_ok, rinv_ok = sem("s_done"), sem("max_ok"), sem("exp_ok"), sem("rinv_ok")
        pt_done, ptr_ok, ptl_ok = sem("pt_done"), sem("ptr_ok"), sem("ptl_ok")
        pv_done, oT_ok, back_done, attn_ok = sem("pv_done"), sem("oT_ok"), sem("back_done"), sem("attn_ok")
        resid_ok, bn1_ok, mv1_ok = sem("resid_ok"), sem("bn1_ok"), sem("mv1_ok")
        var1_ok, rstd1_ok, centre1_ok, x1_ok = sem("var1_ok"), sem("rstd1_ok"), sem("centre1_ok"), sem("x1_ok")
        x1T_done, x1Tr_ok, x1Tl_ok = sem("x1T_done"), sem("x1Tr_ok"), sem("x1Tl_ok")
        wfr_ok, wfl_ok, consts_ok = sem("wfr_ok"), sem("wfl_ok"), sem("consts_ok")
        low_sum_ok, low_all, low_flag_ok = sem("low_sum_ok"), sem("low_all"), sem("low_flag_ok")
        gate_done, up_done, gate_ok = sem("gate_done"), sem("up_done"), sem("gate_ok")
        h0_ok, h0r_ok, h0l_dve, h0l_pool = sem("h0_ok"), sem("h0r_ok"), sem("h0l_dve"), sem("h0l_pool")
        h1_done, h1r_ok, h1f_ok, h1l_ok = sem("h1_done"), sem("h1r_ok"), sem("h1f_ok"), sem("h1l_ok")
        h2_done, h2r_ok, h2f_ok, h2l_ok = sem("h2_done"), sem("h2r_ok"), sem("h2f_ok"), sem("h2l_ok")
        y_done, yT_ok, yn_done = sem("y_done"), sem("yT_ok"), sem("yn_done")
        z_ok, bn2_ok, mv2_ok, var2_ok, rstd2_ok, out_ok = (
            sem("z_ok"), sem("bn2_ok"), sem("mv2_ok"), sem("var2_ok"), sem("rstd2_ok"), sem("out_ok"))

        block = ctx.enter_context(nc.Block())

        @block.sync
        def _(sp):
            sp.sem_inc(out_stored, 16)
            sp.dma_start(w32[:], wqkv).then_inc(wqkv_in, 16)
            for t in range(NT):
                sp.dma_start(xt32[:, TILE * t:TILE * (t + 1)], xT[:, TILE * t:TILE * (t + 1)]).then_inc(xT_in[t], 16)
                if t == 0:
                    sp.dma_start(vec[:], vecs).then_inc(small_in, 16)
                    sp.dma_start(bvb[:], bv.broadcast_to([P, D])).then_inc(small_in, 16)
            sp.dma_start(ident[:], eye).then_inc(eye_in, 16)
            sp.dma_start(xn[:], x).then_inc(x_in, 16)
            for n in range(WCH):
                if n >= RAW_SLOTS:
                    sp.wait_ge(wfl_ok, n - RAW_SLOTS + 1)
                sp.dma_start(raw[:, n % RAW_SLOTS, :], wffn[:, n, :]).then_inc(raw_in[n % RAW_SLOTS], 16)
            with sp.Fori(0, NT) as t:
                sp.wait_ge(out_ok, t + 1)
                sp.dma_start(out[:, bass.ts(t, 4), :], z).then_inc(out_stored, 16)
            sp.wait_ge(out_stored, 16 * NT + 16)

        @block.tensor
        def _(pe):
            pe.sem_inc(h2_done, 1)
            pe.sem_inc(y_done, 1)
            pe.sem_inc(yn_done, 1)

            def split_product(dst, lhs, rhs, first, last):
                (ar, al), (br, bl) = lhs, rhs
                nc.tensor.matmul(dst, ar, br, start=first, stop=False)
                nc.tensor.matmul(dst, ar, bl, start=False, stop=False)
                return nc.tensor.matmul(dst, al, br, start=False, stop=last)

            def wcol(w):
                return w_r[:, w, :], w_l[:, w, :]

            pe.wait_ge(wqkv_l, 1)
            for t in range(NT):
                cols = slice(TILE * t, TILE * (t + 1))
                pe.wait_ge(xT_l, t + 1)
                split_product(bank[t], wcol(1), (xt_r[:, cols], xt_l[:, cols]), True, True).then_inc(k_done, 1)
                split_product(bank[4 + t], wcol(0), (xt_r[:, cols], xt_l[:, cols]), True, True).then_inc(q_done, 1)

            def scores(s):
                p, b = s // 2, s // 2 % 2
                q = slice(P * (s % 2), P * (s % 2) + P)
                pe.wait_ge(ql_ok, p + 1)
                if s == 0:
                    pe.wait_ge(kl_ok, 2)
                if s == 1:
                    pe.wait_ge(kl_ok, 4)
                if s >= 2:
                    pe.wait_ge(exp_ok, s - 1)
                for h in range(S // TILE):
                    keys = slice(S * b + TILE * h, S * b + TILE * (h + 1))
                    last = split_product(score[s % 2][:, TILE * h:TILE * (h + 1)],
                                         (q_r[:, p % 2, q], q_l[:, p % 2, q]),
                                         (k_r[:, keys], k_l[:, keys]), True, True)
                last.then_inc(s_done, 1)

            def turn_probs(s):
                pe.wait_ge(exp_ok, s + 1)
                for h in range(2):
                    if s == 0:
                        pe.wait_ge(v32_ok, h + 1)
                    else:
                        pe.wait_ge(ptl_ok, 2 * s - 1 + h)
                    for k in range(4):
                        last = nc.tensor.transpose(pt_ps[h][:, P * k:P * (k + 1)],
                                                   probs[:, s % 2, P * (4 * h + k):P * (4 * h + k + 1)], ident[:])
                    last.then_inc(pt_done, 1)

            def weigh_values(p, h):
                b = p % 2
                pe.wait_ge(ptl_ok, 4 * p + 3 + h)
                if h == 0:
                    if p < 2:
                        pe.wait_ge(vl_ok, 2 * p + 2)
                    if p == 0:
                        pe.wait_ge(v32_ok, 3)
                    else:
                        pe.wait_ge(oT_ok, p)
                for k in range(4 * h, 4 * h + 4):
                    last = split_product(pv_ps[:, 0:256], (v_r[:, KB * b + k, :], v_l[:, KB * b + k, :]),
                                         (pt_r[:, p % 2, k, :], pt_l[:, p % 2, k, :]), k == 0, k == KB - 1)
                if h == 1:
                    last.then_inc(pv_done, 1)

            def turn_back(p):
                pe.wait_ge(oT_ok, p + 1)
                if p == 0:
                    pe.wait_ge(v32_ok, 4)
                if p >= 2:
                    pe.wait_ge(x1Tl_ok, p - 1)
                if p:
                    pe.wait_ge(attn_ok, p)
                for u in range(2):
                    last = nc.tensor.transpose(misc_ps[:, D * u:D * (u + 1)], oT[:, p % 2, P * u:P * (u + 1)], ident[:])
                last.then_inc(back_done, 1)

            def turn_x1(p):
                pe.wait_ge(x1_ok, p + 1)
                pe.wait_ge(attn_ok, min(p + 2, PAIRS))
                if p:
                    pe.wait_ge(x1Tl_ok, p)
                for u in range(2):
                    last = nc.tensor.transpose(misc_ps[:, P * u:P * (u + 1)], xn[:, 2 * p + u, :], ident[:])
                last.then_inc(x1T_done, 1)

            scores(0)
            scores(1)
            for t in range(NT):
                pe.wait_ge(q32_ok, t + 1)
                for n in range(4):
                    blk = slice(TILE * t + P * n, TILE * t + P * (n + 1))
                    last = split_product(bank[4 + t][:, D * n:D * (n + 1)], (xt_r[:, blk], xt_l[:, blk]), wcol(2), True, True)
                last.then_inc(v_done, 1)
            pe.wait_ge(eye_in, 16)
            for s in range(STEPS + 2):
                if s < STEPS:
                    turn_probs(s)
                if s + 2 < STEPS:
                    scores(s + 2)
                if s >= 4 and s % 2 == 0:
                    turn_back((s - 4) // 2)
                if s >= 2:
                    weigh_values((s - 2) // 2, s % 2)
                if s >= 7 and s % 2 == 1:
                    turn_x1((s - 7) // 2)
                if s == STEPS - 1:
                    pe.wait_ge(low_sum_ok, WCH)
                    pe.wait_ge(consts_ok, 3)
                    nc.tensor.matmul(bank[0][0:1, 0:WCH], ones[:], low_sum[:], start=True, stop=True).then_inc(low_all, 1)
            turn_back(PAIRS - 1)
            pe.wait_ge(low_flag_ok, 1)
            has_low = pe.value_load(low_flag[0:1, 0:1], min_val=0, max_val=2**31 - 1)

            def ffn(low):

                def ffn_product(dst, lhs, rhs, first, last):
                    (ar, al), (br, bl) = lhs, rhs
                    nc.tensor.matmul(dst, ar, br, start=first, stop=False)
                    if low:
                        nc.tensor.matmul(dst, al, br, start=False, stop=False)
                    return nc.tensor.matmul(dst, ar, bl, start=False, stop=last)

                def gated(t):
                    for c in range(HC):
                        feats = slice(P * c, P * (c + 1))
                        cols = bass.ts(t, TILE)
                        for which, dst, done, free in ((W1, gate_ps, gate_done, gate_ok), (W2, up_ps, up_done, h0_ok)):
                            pe.wait_ge(free, HC * t + c + 1)
                            ffn_product(dst[c % 2], (wf_r[:, which, feats], wf_l[:, which, feats]),
                                          (xt_r[:, cols], xt_l[:, cols]), True, True).then_inc(done, 1)

                pe.wait_ge(wfl_ok, W3 + 1)
                pe.wait_ge(x1Tl_ok, PAIRS - 2)
                with pe.Fori(0, NT - 1) as t:
                    gated(t)
                for p in range(PAIRS - 2, PAIRS):
                    turn_x1(p)
                pe.wait_ge(x1Tl_ok, PAIRS)
                gated(NT - 1)

                def hidden1(t, c):
                    pe.wait_ge(h1f_ok, HC * t + c + 1)
                    for k in range(HC):
                        last = ffn_product(h1_ps[c % 2], (wf_r[:, H1 + k, P * c:P * (c + 1)], wf_l[:, H1 + k, P * c:P * (c + 1)]),
                                             (h0_r[:, t, k, :], h0_l[:, t, k, :]), k == 0, k == HC - 1)
                    last.then_inc(h1_done, 1)

                def hidden2(t, c):
                    pe.wait_ge(h2f_ok, HC * t + c + 1)
                    for k in range(HC):
                        if c == 0:
                            pe.wait_ge(h1l_ok, HC * t + k + 1 + BUFS)
                        last = ffn_product(h2_ps[c % 2], (wf_r[:, H2 + k, P * c:P * (c + 1)], wf_l[:, H2 + k, P * c:P * (c + 1)]),
                                             (h1_r[:, k, :], h1_l[:, k, :]), k == 0, k == HC - 1)
                    last.then_inc(h2_done, 1)

                def project(t):
                    pe.wait_ge(yT_ok, t + 1)
                    for k in range(HC):
                        pe.wait_ge(h2l_ok, HC * t + k + 1 + BUFS)
                        last = ffn_product(y_ps, (wf_r[:, W3, P * k:P * (k + 1)], wf_l[:, W3, P * k:P * (k + 1)]),
                                             (h2_r[:, k, :], h2_l[:, k, :]), k == 0, k == HC - 1)
                    last.then_inc(y_done, 1)

                def turn_y(t):
                    pe.wait_ge(yT_ok, t + 2)
                    pe.wait_ge(z_ok, t + 1)
                    for j in range(4):
                        last = nc.tensor.transpose(yn_ps[:, D * j:D * (j + 1)], yT[:, P * j:P * (j + 1)], ident[:])
                    last.then_inc(yn_done, 1)

                pe.wait_ge(wfl_ok, WCH)
                pe.wait_ge(h0l_dve, 2 + BUFS)
                pe.wait_ge(h0l_pool, 2 + BUFS)
                for c in range(HC):
                    hidden1(0, c)
                pe.wait_ge(h0l_dve, 2 * NT + BUFS)
                pe.wait_ge(h0l_pool, 2 * NT + BUFS)

                def tile_body(t, ahead):
                    for c in range(HC):
                        hidden2(t, c)
                    if ahead:
                        hidden1(t + 1, 0)
                        hidden1(t + 1, 1)
                    project(t)
                    if ahead:
                        hidden1(t + 1, 2)
                        hidden1(t + 1, 3)
                    turn_y(t)

                with pe.Fori(0, NT - 1) as t:
                    tile_body(t, True)
                tile_body(NT - 1, False)

            with pe.If(has_low != 0):
                ffn(True)
            with pe.Else():
                ffn(False)

        @block.scalar
        def _(act):
            for s in (gate_ok, h1f_ok, h2f_ok):
                act.sem_inc(s, BUFS)
            act.sem_inc(yT_ok, 1)

            for t in range(NT):
                act.wait_ge(xT_in[t], 16)
                nc.scalar.copy(xt_r[:, TILE * t:TILE * (t + 1)], xt32[:, TILE * t:TILE * (t + 1)]).then_inc(xT_r, 1)
            act.wait_ge(small_in, 32)
            act.wait_ge(bqs_ok, 1)
            for t in range(NT):
                cols = slice(TILE * t, TILE * (t + 1))
                act.wait_ge(k_done, t + 1)
                nc.scalar.activation(k_r[:, cols], bank[t], ACT.Identity, bias=vec[:, BK:BK + 1]).then_inc(kr_ok, 1)
                act.wait_ge(q_done, t + 1)
                nc.scalar.activation(q32[:, cols], bank[4 + t], ACT.Identity, bias=bqs[:], scale=SCALE).then_inc(q32_ok, 1)

            def soften(s):
                act.wait_ge(max_ok, s + 1)
                if s >= 2:
                    act.wait_ge(pt_done, 2 * s - 2)
                nc.scalar.activation(probs[:, s % 2, :], score[s % 2], ACT.Exp, bias=negmax[:, s:s + 1],
                                     accum_out=rowsum[:, s:s + 1]).then_inc(exp_ok, 1)

            def round_v(t):
                act.wait_ge(v32_ok, t + 1)
                nc.scalar.copy(v_r[:, 4 * t:4 * t + 4, :], xt32[:, TILE * t:TILE * (t + 1)].rearrange("p (n d) -> p n d", d=D)).then_inc(vr_ok, 1)

            def round_probs(s, h):
                p = s // 2
                act.wait_ge(pt_done, 2 * s + h + 1)
                if p >= 2:
                    act.wait_ge(pv_done, p - 1)
                nc.scalar.copy(pt_r[:, p % 2, 4 * h:4 * h + 4, P * (s % 2):P * (s % 2) + P],
                               pt_ps[h].rearrange("p (k q) -> p k q", q=P)).then_inc(ptr_ok, 1)

            def sum_low(n):
                act.wait_ge(wfl_ok, n + 1)
                if n:
                    act.wait_ge(low_sum_ok, n)
                nc.scalar.activation(low_abs[:], wf_l[:, n, :].bitcast(F32), ACT.Abs, scale=2.0 ** 64,
                                     accum_out=low_sum[:, n:n + 1]).then_inc(low_sum_ok, 1)

            def take_oT(p):
                act.wait_ge(pv_done, p + 1)
                if p >= 2:
                    act.wait_ge(back_done, p - 1)
                nc.scalar.copy(oT[:, p % 2, :], pv_ps[:, 0:256]).then_inc(oT_ok, 1)

            def divide(p):
                act.wait_ge(back_done, p + 1)
                act.wait_ge(rinv_ok, p + 1)
                if p >= 2:
                    act.wait_ge(resid_ok, p - 1)
                for u in range(2):
                    last = nc.scalar.activation(attn[:, p % 2, u, :], misc_ps[:, D * u:D * (u + 1)], ACT.Identity,
                                                scale=rinv[:, 2 * p + u:2 * p + u + 1])
                last.then_inc(attn_ok, 1)

            def round_x1(p):
                act.wait_ge(x1T_done, p + 1)
                nc.scalar.copy(xt_r[:, 256 * p:256 * (p + 1)], misc_ps[:, 0:256]).then_inc(x1Tr_ok, 1)

            soften(0)
            round_v(0)
            round_v(1)
            for s in range(STEPS + 2):
                if s >= 4 and s % 2 == 0:
                    take_oT((s - 4) // 2)
                if s >= 5 and s % 2 == 1:
                    divide((s - 5) // 2)
                if s >= 8 and s % 2 == 0:
                    round_x1((s - 8) // 2)
                if s < STEPS:
                    round_probs(s, 0)
                    round_probs(s, 1)
                if s + 1 < STEPS:
                    soften(s + 1)
                if s == 0:
                    round_v(2)
                    round_v(3)
                if 4 <= s < 4 + WCH:
                    sum_low(s - 4)
            take_oT(PAIRS - 1)
            round_x1(PAIRS - 3)
            divide(PAIRS - 1)
            nc.scalar.preload_act_table(ACT.Silu)

            def silu(t, c):
                act.wait_ge(gate_done, HC * t + c + 1)
                act.wait_ge(h0_ok, HC * t + c + 1)
                nc.scalar.activation(gate[:, c % 2, :], gate_ps[c % 2], ACT.Silu, scale=vec[:, S1 + c:S1 + c + 1]).then_inc(gate_ok, 1)

            def round_h0(t, c):
                act.wait_ge(h0_ok, HC * t + c + 1 + BUFS)
                nc.scalar.copy(h0_r[:, t, c, :], h32[:, c, :]).then_inc(h0r_ok, 1)

            def gated(t):
                silu(t, 0)
                silu(t, 1)
                for c in range(HC):
                    round_h0(t, c)
                    if c + 2 < HC:
                        silu(t, c + 2)

            with act.Fori(0, NT - 1) as t:
                gated(t)
            for p in range(PAIRS - 2, PAIRS):
                round_x1(p)
            gated(NT - 1)

            def gelu(t, c, psum, done, value, scale, dst_r, r_ok, f_ok, l_ok, slot):
                act.wait_ge(done, value)
                nc.scalar.activation(dst_r[:, c, :], psum[c % 2], ACT.Gelu, scale=vec[:, scale + c:scale + c + 1]).then_inc(r_ok, 1)
                act.wait_ge(l_ok, HC * t + c + 1)
                nc.scalar.activation(h32[:, slot + c % 2, :], psum[c % 2], ACT.Gelu, scale=vec[:, scale + c:scale + c + 1]).then_inc(f_ok, 1)

            def gelu1(t, c):
                if c == 0:
                    act.wait_ge(h2_done, HC * t + 1)
                gelu(t, c, h1_ps, h1_done, HC * t + c + 1, HS1, h1_r, h1r_ok, h1f_ok, h1l_ok, 0)

            def gelu2(t, c):
                if c == 0:
                    act.wait_ge(y_done, t + 1)
                gelu(t, c, h2_ps, h2_done, HC * t + c + 2, HS2, h2_r, h2r_ok, h2f_ok, h2l_ok, 2)

            def take_y(t):
                act.wait_ge(y_done, t + 2)
                act.wait_ge(yn_done, t + 1)
                nc.scalar.activation(yT, y_ps, ACT.Identity, scale=vec[:, S3:S3 + 1]).then_inc(yT_ok, 1)

            def tile_body(t, ahead):
                for c in range(HC):
                    gelu2(t, c)
                if ahead:
                    gelu1(t + 1, 0)
                    gelu1(t + 1, 1)
                take_y(t)
                if ahead:
                    gelu1(t + 1, 2)
                    gelu1(t + 1, 3)

            nc.scalar.preload_act_table(ACT.Gelu)
            act.wait_ge(h0l_dve, 2 * NT + BUFS)
            act.wait_ge(h0l_pool, 2 * NT + BUFS)
            for c in range(HC):
                gelu1(0, c)
            with act.Fori(0, NT - 1) as t:
                tile_body(t, True)
            tile_body(NT - 1, False)

        @block.vector
        def _(dve):
            for s in (h0_ok, h0l_dve, h1l_ok, h2l_ok):
                dve.sem_inc(s, BUFS)
            dve.sem_inc(z_ok, 1)

            dve.wait_ge(wqkv_in, 16)
            nc.vector.tensor_copy(w_r, w32[:]).then_inc(wqkv_r, 1)
            dve.wait_ge(wqkv_r, 1)
            nc.vector.tensor_tensor(w_l, w32[:], w_r.bitcast(F32), ALU.subtract).then_inc(wqkv_l, 1)

            def split_xT(t):
                cols = slice(TILE * t, TILE * (t + 1))
                dve.wait_ge(xT_r, t + 1)
                nc.vector.tensor_tensor(xt_l[:, cols], xt32[:, cols], xt_r[:, cols].bitcast(F32), ALU.subtract).then_inc(xT_l, 1)

            def split_k(t):
                cols = slice(TILE * t, TILE * (t + 1))
                dve.wait_ge(kr_ok, t + 1)
                nc.vector.scalar_tensor_tensor(out=k_l[:, cols], in0=bank[t], scalar=vec[:, BK:BK + 1],
                                               in1=k_r[:, cols].bitcast(F32), op0=ALU.add, op1=ALU.subtract).then_inc(kl_ok, 1)

            split_xT(0)
            dve.wait_ge(small_in, 32)
            nc.vector.tensor_scalar(bqs[:], vec[:, BQ:BQ + 1], SCALE, None, ALU.mult).then_inc(bqs_ok, 1)
            for t in range(1, NT):
                split_xT(t)
            for t in range(NT):
                split_k(t)

            def row_max(s):
                dve.wait_ge(s_done, s + 1)
                nc.vector.tensor_reduce(negmax[:, s:s + 1], score[s % 2], AX.X, ALU.max, negate=True).then_inc(max_ok, 1)

            def bias_v(t):
                dve.wait_ge(v_done, t + 1)
                dst = xt32[:, TILE * t:TILE * (t + 1)].rearrange("p (n d) -> p n d", d=D)
                src = bank[4 + t].rearrange("p (n d) -> p n d", d=D)
                nc.vector.tensor_tensor(dst, src, bvb[:].unsqueeze(1).broadcast_to([P, 4, D]), ALU.add).then_inc(v32_ok, 1)

            def split_probs(s, h):
                p = s // 2
                dve.wait_ge(ptr_ok, 2 * s + h + 1)
                q = slice(P * (s % 2), P * (s % 2) + P)
                nc.vector.tensor_tensor(pt_l[:, p % 2, 4 * h:4 * h + 4, q], pt_ps[h].rearrange("p (k q) -> p k q", q=P),
                                        pt_r[:, p % 2, 4 * h:4 * h + 4, q].bitcast(F32), ALU.subtract).then_inc(ptl_ok, 1)

            def invert_sums(p):
                dve.wait_ge(exp_ok, 2 * p + 2)
                nc.vector.reciprocal(rinv[:, 2 * p:2 * p + 2], rowsum[:, 2 * p:2 * p + 2]).then_inc(rinv_ok, 1)

            def stats1(p):
                dve.wait_ge(resid_ok, p + 1)
                for u in range(2):
                    nc.vector.bn_stats(bn6[:, u, :], xn[:, 2 * p + u, :]).then_inc(bn1_ok, 1)
                for u in range(2):
                    dve.wait_ge(bn1_ok, 2 * p + u + 1)
                    last = nc.vector.bn_aggr(mv1[:, 2 * p + u, :], bn6[:, u, :])
                last.then_inc(mv1_ok, 1)

            def normalise1(p):
                dve.wait_ge(rstd1_ok, p + 1)
                for s in (2 * p, 2 * p + 1):
                    last = nc.vector.tensor_scalar(xn[:, s, :], xn[:, s, :], mv1[:, s, 0:1], rstd1[:, s:s + 1], ALU.subtract, ALU.mult)
                last.then_inc(x1_ok, 1)

            def split_x1(p):
                dve.wait_ge(x1Tr_ok, p + 1)
                nc.vector.tensor_tensor(xt_l[:, 256 * p:256 * (p + 1)], misc_ps[:, 0:256],
                                        xt_r[:, 256 * p:256 * (p + 1)].bitcast(F32), ALU.subtract).then_inc(x1Tl_ok, 1)

            def round_weights(n):
                dve.wait_ge(raw_in[n % RAW_SLOTS], 16 * (n // RAW_SLOTS + 1))
                nc.vector.tensor_copy(wf_r[:, n, :], raw[:, n % RAW_SLOTS, :]).then_inc(wfr_ok, 1)

            row_max(0)
            bias_v(0)
            bias_v(1)
            row_max(1)
            bias_v(2)
            bias_v(3)
            for s in range(STEPS + 2):
                if s >= 8 and s % 2 == 0:
                    split_x1((s - 8) // 2)
                if s < STEPS:
                    split_probs(s, 0)
                    split_probs(s, 1)
                if s + 2 < STEPS:
                    row_max(s + 2)
                if s % 2 == 1 and s < STEPS:
                    invert_sums(s // 2)
                if s >= 6 and s % 2 == 0:
                    stats1((s - 6) // 2)
                if s == STEPS + 1:
                    stats1(PAIRS - 2)
                if 2 <= s < 2 + WCH:
                    round_weights(s - 2)
                if s == STEPS:
                    dve.wait_ge(low_all, 1)
                    nc.vector.tensor_reduce(low_flag[:].bitcast(F32), bank[0][0:1, 0:WCH], AX.X, ALU.add).then_inc(low_flag_ok, 1)
            split_x1(PAIRS - 3)
            normalise1(PAIRS - 2)
            stats1(PAIRS - 1)
            normalise1(PAIRS - 1)

            def gated(t, c):
                dve.wait_ge(up_done, HC * t + c + 1)
                dve.wait_ge(gate_ok, HC * t + c + 1 + BUFS)
                dve.wait_ge(h0l_dve if c % 2 == 0 else h0l_pool, 2 * t + c // 2 + 1)
                nc.vector.scalar_tensor_tensor(out=h32[:, c, :], in0=up_ps[c % 2], scalar=vec[:, S2 + c:S2 + c + 1],
                                               in1=gate[:, c % 2, :], op0=ALU.mult, op1=ALU.mult).then_inc(h0_ok, 1)

            def split_h0(t, c):
                dve.wait_ge(h0r_ok, HC * t + c + 1)
                nc.vector.tensor_tensor(h0_l[:, t, c, :], h32[:, c, :], h0_r[:, t, c, :].bitcast(F32), ALU.subtract).then_inc(h0l_dve, 1)

            def gated_tile(t):
                gated(t, 0)
                gated(t, 1)
                split_h0(t, 0)
                gated(t, 2)
                gated(t, 3)
                split_h0(t, 2)

            with dve.Fori(0, NT - 1) as t:
                gated_tile(t)
            for p in range(PAIRS - 2, PAIRS):
                split_x1(p)
            gated_tile(NT - 1)

            def split_h(t, c, f_ok, slot, dst_r, dst_l, l_ok):
                dve.wait_ge(f_ok, HC * t + c + 1 + BUFS)
                nc.vector.tensor_tensor(dst_l[:, c, :], h32[:, slot + c % 2, :], dst_r[:, c, :].bitcast(F32), ALU.subtract).then_inc(l_ok, 1)

            def split_h1(t, c):
                split_h(t, c, h1f_ok, 0, h1_r, h1_l, h1l_ok)

            def split_h2(t, c):
                split_h(t, c, h2f_ok, 2, h2_r, h2_l, h2l_ok)

            def finish(t):
                dve.wait_ge(yn_done, t + 2)
                dve.wait_ge(out_stored, 16 * t + 16)
                nc.vector.tensor_tensor(z, yn_ps.rearrange("p (j d) -> p j d", d=D),
                                        xn[:, bass.ts(t, 4), :], ALU.add).then_inc(z_ok, 1)
                dve.wait_ge(z_ok, t + 2)
                for j in range(4):
                    last = nc.vector.bn_stats(bn6[:, j, :], z[:, j, :])
                dve.drain()
                for j in range(4):
                    last = nc.vector.bn_aggr(mv2[:, j, :], bn6[:, j, :])
                last.then_inc(mv2_ok, 1)
                dve.wait_ge(rstd2_ok, t + 1)
                for j in range(4):
                    last = nc.vector.tensor_scalar(z[:, j, :], z[:, j, :], mv2[:, j, 0:1], rstd2[:, j:j + 1], ALU.subtract, ALU.mult)
                last.then_inc(out_ok, 1)

            def tile_body(t, ahead):
                for c in range(HC):
                    split_h2(t, c)
                if ahead:
                    for c in range(HC):
                        split_h1(t + 1, c)
                finish(t)

            for c in range(HC):
                split_h1(0, c)
            with dve.Fori(0, NT - 1) as t:
                tile_body(t, True)
            tile_body(NT - 1, False)

        @block.gpsimd
        def _(pool):
            pool.sem_inc(h0l_pool, BUFS)
            nc.gpsimd.memset(mhalf[:], -0.5).then_inc(consts_ok, 1)
            nc.gpsimd.memset(eps[:], EPS).then_inc(consts_ok, 1)
            nc.gpsimd.memset(ones[:], 1.0).then_inc(consts_ok, 1)

            def split_q(p):
                i, b = p // 2, p % 2
                src = q32[:, S * b + 256 * i:S * b + 256 * (i + 1)]
                if p < 4:
                    pool.wait_ge(q32_ok, 2 * b + i // 2 + 1)
                if p >= 2:
                    pool.wait_ge(s_done, 2 * p - 2)
                nc.gpsimd.tensor_copy(q_r[:, p % 2, :], src).then_inc(qr_ok, 1)
                pool.wait_ge(qr_ok, p + 1)
                nc.gpsimd.tensor_tensor(q_l[:, p % 2, :], src, q_r[:, p % 2, :].bitcast(F32), ALU.subtract).then_inc(ql_ok, 1)

            def split_v(t):
                pool.wait_ge(vr_ok, t + 1)
                src = xt32[:, TILE * t:TILE * (t + 1)].rearrange("p (n d) -> p n d", d=D)
                nc.gpsimd.tensor_tensor(v_l[:, 4 * t:4 * t + 4, :], src, v_r[:, 4 * t:4 * t + 4, :].bitcast(F32), ALU.subtract).then_inc(vl_ok, 1)

            def add_residual(p):
                pool.wait_ge(attn_ok, p + 1)
                if p == 0:
                    pool.wait_ge(x_in, 16)
                nc.gpsimd.tensor_tensor(xn[:, 2 * p:2 * p + 2, :], attn[:, p % 2, :, :], xn[:, 2 * p:2 * p + 2, :], ALU.add).then_inc(resid_ok, 1)

            def normalise1(p):
                two = slice(2 * p, 2 * p + 2)
                pool.wait_ge(mv1_ok, p + 1)
                nc.gpsimd.tensor_scalar(rstd1[:, two], mv1[:, two, 1], EPS, None, ALU.add).then_inc(var1_ok, 1)
                pool.wait_ge(var1_ok, p + 1)
                pool.wait_ge(consts_ok, 3)
                nc.gpsimd.tensor_tensor(rstd1[:, two], rstd1[:, two], mhalf[:, 0:2], ALU.pow).then_inc(rstd1_ok, 1)
                if p < PAIRS - 2:
                    nc.gpsimd.tensor_tensor(xn[:, two, :], xn[:, two, :], mv1[:, two, 0:1].broadcast_to([P, 2, D]), ALU.subtract).then_inc(centre1_ok, 1)
                    pool.wait_ge(rstd1_ok, p + 1)
                    pool.wait_ge(centre1_ok, p + 1)
                    nc.gpsimd.tensor_tensor(xn[:, two, :], xn[:, two, :], rstd1[:, two].unsqueeze(2).broadcast_to([P, 2, D]), ALU.mult).then_inc(x1_ok, 1)

            def split_weights(n):
                pool.wait_ge(wfr_ok, n + 1)
                nc.gpsimd.tensor_tensor(wf_l[:, n, :], raw[:, n % RAW_SLOTS, :], wf_r[:, n, :].bitcast(F32), ALU.subtract).then_inc(wfl_ok, 1)

            split_q(0)
            split_q(1)
            for t in range(NT):
                split_v(t)
            for s in range(STEPS + 2):
                if s % 2 == 0 and s // 2 + 2 < PAIRS:
                    split_q(s // 2 + 2)
                if s >= 5 and s % 2 == 1:
                    add_residual((s - 5) // 2)
                if s >= 6 and s % 2 == 0:
                    normalise1((s - 6) // 2)
                if 2 <= s < 2 + WCH:
                    split_weights(s - 2)
            normalise1(PAIRS - 2)
            add_residual(PAIRS - 1)
            normalise1(PAIRS - 1)

            def split_h0(t, c):
                pool.wait_ge(h0r_ok, HC * t + c + 1)
                nc.gpsimd.tensor_tensor(h0_l[:, t, c, :], h32[:, c, :], h0_r[:, t, c, :].bitcast(F32), ALU.subtract).then_inc(h0l_pool, 1)

            with pool.Fori(0, NT) as t:
                split_h0(t, 1)
                split_h0(t, 3)

            with pool.Fori(0, NT) as t:
                pool.wait_ge(mv2_ok, t + 1)
                nc.gpsimd.tensor_tensor(rstd2[:], mv2[:, :, 1], eps[:], ALU.add).then_inc(var2_ok, 1)
                pool.wait_ge(var2_ok, t + 1)
                nc.gpsimd.tensor_tensor(rstd2[:], rstd2[:], mhalf[:], ALU.pow).then_inc(rstd2_ok, 1)


def kernel(L0_attn_X, L0_attn_W_q, L0_attn_W_k, L0_attn_W_v, L0_attn_b_q, L0_attn_b_k, L0_attn_b_v,
           L0_ffn_w1_w, L0_ffn_w1_s, L0_ffn_w2_w, L0_ffn_w2_s, L0_ffn_h1_w, L0_ffn_h1_s,
           L0_ffn_h2_w, L0_ffn_h2_s, L0_ffn_w3_w, L0_ffn_w3_s):
    import numpy as np
    import concourse.bacc as bacc
    from concourse.bass_utils import run_bass_kernel_spmd

    def chunked(w):
        wt = np.asarray(w).T
        return wt.reshape(-1, P, wt.shape[1]).transpose(1, 0, 2)

    def column(v):
        return np.asarray(v).reshape(-1, P).T

    x = np.ascontiguousarray(L0_attn_X)
    arrays = {
        "x": np.ascontiguousarray(x.reshape(B, NT, 2, P, D).transpose(3, 1, 0, 2, 4)).reshape(P, STEPS, D),
        "xT": np.ascontiguousarray(x.reshape(B * S, D).T),
        "wqkv": np.ascontiguousarray(np.stack([L0_attn_W_q, L0_attn_W_k, L0_attn_W_v], axis=1)),
        "bv": np.ascontiguousarray(L0_attn_b_v).reshape(1, D),
        "vecs": np.ascontiguousarray(np.concatenate([column(v) for v in (
            L0_attn_b_q, L0_attn_b_k, L0_ffn_w1_s, L0_ffn_w2_s, L0_ffn_h1_s, L0_ffn_h2_s, L0_ffn_w3_s)], axis=1)),
        "wffn": np.ascontiguousarray(np.concatenate(
            [chunked(L0_ffn_w1_w), chunked(L0_ffn_w2_w), chunked(L0_ffn_w3_w).reshape(P, 1, HID),
             chunked(L0_ffn_h1_w), chunked(L0_ffn_h2_w)], axis=1)),
        "eye": np.eye(P, dtype=np.float32),
    }
    nc = bacc.Bacc("TRN2", target_bir_lowering=False, num_devices=1)
    args = [nc.dram_tensor(n, arrays[n].shape, mybir.dt.from_np(arrays[n].dtype), kind="ExternalInput").ap()
            for n in ("xT", "x", "wqkv", "bv", "vecs", "wffn", "eye")]
    args.append(nc.dram_tensor("out", (P, STEPS, D), F32, kind="ExternalOutput").ap())
    build(nc, *args)
    r = run_bass_kernel_spmd(nc, [arrays], core_ids=[0])
    by_step = r.results[0]["out"].reshape(P, NT, B, 2, D)
    return np.ascontiguousarray(by_step.transpose(2, 1, 3, 0, 4)).reshape(B, S, D)
```

```python
from contextlib import ExitStack

import concourse.bass as bass
from concourse import mybir

F32 = mybir.dt.float32
F32R = mybir.dt.float32r
ALU = mybir.AluOpType
ACT = mybir.ActivationFunctionType
AX = mybir.AxisListType

P = 128
B, S, D = 2, 1024, 128
HID = 512
TILE = 512
NT = B * S // TILE
STEPS = B * S // P
PAIRS = STEPS // 2
KB = S // P
HC = HID // P
SCALE = D ** -0.5
EPS = 1e-5

W1, W2, W3, H1, H2 = 0, 1, 2, 3, 3 + HC
WCH = H2 + HC
RAW_SLOTS = 4

BUFS = 2

BQ, BK, S1, S2, HS1, HS2, S3 = 0, 1, 2, 2 + HC, 2 + 2 * HC, 2 + 3 * HC, 2 + 4 * HC
VECS = S3 + 1


def build(nc, xT, x, wqkv, bv, vecs, wffn, eye, out):
    with ExitStack() as ctx:
        def sb(name, shape, dt):
            return ctx.enter_context(nc.sbuf_tensor(name, shape, dt))

        def ps(name, shape):
            return ctx.enter_context(nc.psum_tensor(name, shape, F32))

        def sem(name):
            return ctx.enter_context(nc.semaphore(name))

        arena_a = sb("arena_a", [P, 16384], F32R)
        arena_b = sb("arena_b", [P, 5888], F32R)
        arena_c = sb("arena_c", [P, 6144], F32)
        pt_r = arena_a[:, 0:4096].rearrange("p (a k q) -> p a k q", a=2, k=KB)
        pt_l = arena_a[:, 4096:8192].rearrange("p (a k q) -> p a k q", a=2, k=KB)
        k_r = arena_a[:, 8192:10240]
        k_l = arena_a[:, 10240:12288]
        v_r = arena_a[:, 12288:14336].rearrange("p (n d) -> p n d", d=D)
        v_l = arena_a[:, 14336:16384].rearrange("p (n d) -> p n d", d=D)
        h1_r = arena_a[:, 0:2048].rearrange("p (c n) -> p c n", c=HC)
        h1_l = arena_a[:, 2048:4096].rearrange("p (c n) -> p c n", c=HC)
        h2_r = arena_a[:, 4096:6144].rearrange("p (c n) -> p c n", c=HC)
        h2_l = arena_a[:, 6144:8192].rearrange("p (c n) -> p c n", c=HC)
        xt_r = arena_b[:, 0:2048]
        xt_l = arena_b[:, 2048:4096]
        q_r = arena_b[:, 4096:4608].rearrange("p (a q) -> p a q", a=2)
        q_l = arena_b[:, 4608:5120].rearrange("p (a q) -> p a q", a=2)
        w_r = arena_b[:, 5120:5504].rearrange("p (w d) -> p w d", w=3)
        w_l = arena_b[:, 5504:5888].rearrange("p (w d) -> p w d", w=3)
        xt32 = arena_c[:, 0:2048]
        q32 = arena_c[:, 2048:4096]
        probs = arena_c[:, 4096:6144].rearrange("p (a k) -> p a k", a=2)
        tanh_g = arena_c[:, 0:1024].rearrange("p (a n) -> p a n", a=BUFS)
        u32 = arena_c[:, 1024:2048].rearrange("p (a n) -> p a n", a=BUFS)
        h0_32 = arena_c[:, 2048:3072].rearrange("p (a n) -> p a n", a=BUFS)
        yT = arena_c[:, 3072:3584]
        z = arena_c[:, 3584:4096].rearrange("p (j d) -> p j d", d=D)
        h32 = arena_c[:, 4096:6144].rearrange("p (a n) -> p a n", a=2 * BUFS)
        h0_r = sb("h0_r", [P, HC, TILE], F32R)
        h0_l = sb("h0_l", [P, HC, TILE], F32R)

        xn = sb("xn", [P, STEPS, D], F32)
        oT = sb("oT", [P, 2, 256], F32)
        attn = sb("attn", [P, 2, 2, D], F32)
        raw = sb("raw", [P, RAW_SLOTS, 512], F32)
        wf_r = sb("wf_r", [P, WCH, 512], F32R)
        wf_l = sb("wf_l", [P, WCH, 512], F32R)
        w32 = sb("w32", [P, 3, D], F32)
        bvb = sb("bvb", [P, D], F32)
        vec = sb("vec", [P, VECS], F32)
        bqs = sb("bqs", [P, 1], F32)
        half_s1 = sb("half_s1", [P, HC], F32)
        half_s1s2 = sb("half_s1s2", [P, HC], F32)
        ident = sb("ident", [P, P], F32)
        negmax = sb("negmax", [P, STEPS], F32)
        rowsum = sb("rowsum", [P, STEPS], F32)
        rinv = sb("rinv", [P, STEPS], F32)
        bn6 = sb("bn6", [P, 4, 6], F32)
        mv1 = sb("mv1", [P, STEPS, 2], F32)
        rstd1 = sb("rstd1", [P, STEPS], F32)
        mv2 = sb("mv2", [P, 4, 2], F32)
        rstd2 = sb("rstd2", [P, 4], F32)
        low_abs = sb("low_abs", [P, 512], F32)
        low_sum = sb("low_sum", [P, WCH], F32)
        low_flag = sb("low_flag", [1, 1], mybir.dt.int32)
        ones = sb("ones", [P, 1], F32)
        mhalf = sb("mhalf", [P, 4], F32)
        eps = sb("eps", [P, 4], F32)

        psum = ps("psum", [P, 8 * TILE])
        bank = [psum[:, TILE * i:TILE * (i + 1)] for i in range(8)]
        score = [psum[:, 2 * TILE * i:2 * TILE * (i + 1)] for i in range(2)]
        pt_ps = [bank[4], bank[5]]
        pv_ps, misc_ps = bank[6], bank[7]
        gate_ps, up_ps = bank[0], bank[1]
        h2_ps, h1_ps = [bank[2], bank[3]], [bank[4], bank[5]]
        y_ps, yn_ps = bank[6], bank[7]
        x1T_ps = [bank[3] if p in (PAIRS - 3, PAIRS - 2) else misc_ps for p in range(PAIRS)]

        xT_in = [sem(f"xT_in{t}") for t in range(NT)]
        wqkv_in, small_in, x_in, eye_in, out_stored = (
            sem("wqkv_in"), sem("small_in"), sem("x_in"), sem("eye_in"), sem("out_stored"))
        raw_in = [sem(f"raw_in{n}") for n in range(RAW_SLOTS)]
        wqkv_r, wqkv_l, bqs_ok = sem("wqkv_r"), sem("wqkv_l"), sem("bqs_ok")
        xT_r, xT_l = sem("xT_r"), sem("xT_l")
        k_done, q_done, v_done = sem("k_done"), sem("q_done"), sem("v_done")
        kr_ok, kl_ok, q32_ok = sem("kr_ok"), sem("kl_ok"), sem("q32_ok")
        v32_ok, vr_ok, vl_ok = sem("v32_ok"), sem("vr_ok"), sem("vl_ok")
        qr_ok, ql_ok = sem("qr_ok"), sem("ql_ok")
        s_done, max_ok, exp_ok, rinv_ok = sem("s_done"), sem("max_ok"), sem("exp_ok"), sem("rinv_ok")
        pt_done, ptr_ok, ptl_ok = sem("pt_done"), sem("ptr_ok"), sem("ptl_ok")
        pv_done, oT_ok, back_done, attn_ok = sem("pv_done"), sem("oT_ok"), sem("back_done"), sem("attn_ok")
        resid_ok, bn1_ok, mv1_ok = sem("resid_ok"), sem("bn1_ok"), sem("mv1_ok")
        var1_ok, rstd1_ok, centre1_ok, x1_ok = sem("var1_ok"), sem("rstd1_ok"), sem("centre1_ok"), sem("x1_ok")
        x1T_done, x1Tr_ok, x1Tl_ok = sem("x1T_done"), sem("x1Tr_ok"), sem("x1Tl_ok")
        wfr_ok, wfl_ok, consts_ok = sem("wfr_ok"), sem("wfl_ok"), sem("consts_ok")
        low_sum_ok, low_all, low_flag_ok = sem("low_sum_ok"), sem("low_all"), sem("low_flag_ok")
        half_s_ok, gate_done, up_done = sem("half_s_ok"), sem("gate_done"), sem("up_done")
        tanh_ok, u_ok = sem("tanh_ok"), sem("u_ok")
        h0_ok, h0r_ok, h0l_dve, h0l_pool = sem("h0_ok"), sem("h0r_ok"), sem("h0l_dve"), sem("h0l_pool")
        h1_done, h1r_ok, h1f_ok, h1l_ok = sem("h1_done"), sem("h1r_ok"), sem("h1f_ok"), sem("h1l_ok")
        h2_done, h2r_ok, h2f_ok, h2l_ok = sem("h2_done"), sem("h2r_ok"), sem("h2f_ok"), sem("h2l_ok")
        y_done, yT_ok, yn_done = sem("y_done"), sem("yT_ok"), sem("yn_done")
        z_ok, bn2_ok, mv2_ok, var2_ok, rstd2_ok, out_ok = (
            sem("z_ok"), sem("bn2_ok"), sem("mv2_ok"), sem("var2_ok"), sem("rstd2_ok"), sem("out_ok"))

        block = ctx.enter_context(nc.Block())

        @block.sync
        def _(sp):
            sp.sem_inc(out_stored, 16)
            sp.dma_start(w32[:], wqkv).then_inc(wqkv_in, 16)
            for t in range(NT):
                sp.dma_start(xt32[:, TILE * t:TILE * (t + 1)], xT[:, TILE * t:TILE * (t + 1)]).then_inc(xT_in[t], 16)
                if t == 0:
                    sp.dma_start(vec[:], vecs).then_inc(small_in, 16)
                    sp.dma_start(bvb[:], bv.broadcast_to([P, D])).then_inc(small_in, 16)
            sp.dma_start(ident[:], eye).then_inc(eye_in, 16)
            sp.dma_start(xn[:], x).then_inc(x_in, 16)
            for n in range(WCH):
                if n >= RAW_SLOTS:
                    sp.wait_ge(wfl_ok, n - RAW_SLOTS + 1)
                sp.dma_start(raw[:, n % RAW_SLOTS, :], wffn[:, n, :]).then_inc(raw_in[n % RAW_SLOTS], 16)
            with sp.Fori(0, NT) as t:
                sp.wait_ge(out_ok, t + 1)
                sp.dma_start(out[:, bass.ts(t, 4), :], z).then_inc(out_stored, 16)
            sp.wait_ge(out_stored, 16 * NT + 16)

        @block.tensor
        def _(pe):
            pe.sem_inc(h2_done, 1)
            pe.sem_inc(y_done, 1)
            pe.sem_inc(yn_done, 1)

            def split_product(dst, lhs, rhs, first, last):
                (ar, al), (br, bl) = lhs, rhs
                nc.tensor.matmul(dst, ar, br, start=first, stop=False)
                nc.tensor.matmul(dst, ar, bl, start=False, stop=False)
                return nc.tensor.matmul(dst, al, br, start=False, stop=last)

            def wcol(w):
                return w_r[:, w, :], w_l[:, w, :]

            pe.wait_ge(wqkv_l, 1)
            for t in range(NT):
                cols = slice(TILE * t, TILE * (t + 1))
                pe.wait_ge(xT_l, t + 1)
                split_product(bank[t], wcol(1), (xt_r[:, cols], xt_l[:, cols]), True, True).then_inc(k_done, 1)
                split_product(bank[4 + t], wcol(0), (xt_r[:, cols], xt_l[:, cols]), True, True).then_inc(q_done, 1)

            def scores(s):
                p, b = s // 2, s // 2 % 2
                q = slice(P * (s % 2), P * (s % 2) + P)
                pe.wait_ge(ql_ok, p + 1)
                if s == 0:
                    pe.wait_ge(kl_ok, 2)
                if s == 1:
                    pe.wait_ge(kl_ok, 4)
                if s >= 2:
                    pe.wait_ge(exp_ok, s - 1)
                for h in range(S // TILE):
                    keys = slice(S * b + TILE * h, S * b + TILE * (h + 1))
                    last = split_product(score[s % 2][:, TILE * h:TILE * (h + 1)],
                                         (q_r[:, p % 2, q], q_l[:, p % 2, q]),
                                         (k_r[:, keys], k_l[:, keys]), True, True)
                last.then_inc(s_done, 1)

            def turn_probs(s):
                pe.wait_ge(exp_ok, s + 1)
                for h in range(2):
                    if s == 0:
                        pe.wait_ge(v32_ok, h + 1)
                    else:
                        pe.wait_ge(ptl_ok, 2 * s - 1 + h)
                    for k in range(4):
                        last = nc.tensor.transpose(pt_ps[h][:, P * k:P * (k + 1)],
                                                   probs[:, s % 2, P * (4 * h + k):P * (4 * h + k + 1)], ident[:])
                    last.then_inc(pt_done, 1)

            def weigh_values(p, h):
                b = p % 2
                pe.wait_ge(ptl_ok, 4 * p + 3 + h)
                if h == 0:
                    if p < 2:
                        pe.wait_ge(vl_ok, 2 * p + 2)
                    if p == 0:
                        pe.wait_ge(v32_ok, 3)
                    else:
                        pe.wait_ge(oT_ok, p)
                for k in range(4 * h, 4 * h + 4):
                    last = split_product(pv_ps[:, 0:256], (v_r[:, KB * b + k, :], v_l[:, KB * b + k, :]),
                                         (pt_r[:, p % 2, k, :], pt_l[:, p % 2, k, :]), k == 0, k == KB - 1)
                if h == 1:
                    last.then_inc(pv_done, 1)

            def turn_back(p):
                pe.wait_ge(oT_ok, p + 1)
                if p == 0:
                    pe.wait_ge(v32_ok, 4)
                if p >= 2:
                    pe.wait_ge(x1Tl_ok, p - 1 if p < PAIRS - 1 else p - 2)
                if p:
                    pe.wait_ge(attn_ok, p)
                for u in range(2):
                    last = nc.tensor.transpose(misc_ps[:, D * u:D * (u + 1)], oT[:, p % 2, P * u:P * (u + 1)], ident[:])
                last.then_inc(back_done, 1)

            def turn_x1(p):
                pe.wait_ge(x1_ok, p + 1)
                if x1T_ps[p] is misc_ps:
                    pe.wait_ge(attn_ok, min(p + 2, PAIRS))
                if p and p != PAIRS - 3:
                    pe.wait_ge(x1Tl_ok, p)
                for u in range(2):
                    last = nc.tensor.transpose(x1T_ps[p][:, P * u:P * (u + 1)], xn[:, 2 * p + u, :], ident[:])
                last.then_inc(x1T_done, 1)

            scores(0)
            scores(1)
            for t in range(NT):
                pe.wait_ge(q32_ok, t + 1)
                for n in range(4):
                    blk = slice(TILE * t + P * n, TILE * t + P * (n + 1))
                    last = split_product(bank[4 + t][:, D * n:D * (n + 1)], (xt_r[:, blk], xt_l[:, blk]), wcol(2), True, True)
                last.then_inc(v_done, 1)
            pe.wait_ge(eye_in, 16)

            def attention_step(s):
                if s < STEPS:
                    turn_probs(s)
                if s + 2 < STEPS:
                    scores(s + 2)
                if s >= 4 and s % 2 == 0:
                    turn_back((s - 4) // 2)
                if s >= 2:
                    weigh_values((s - 2) // 2, s % 2)
                if s >= 7 and s % 2 == 1:
                    turn_x1((s - 7) // 2)

            for s in range(STEPS - 3):
                attention_step(s)
            pe.wait_ge(exp_ok, STEPS - 2)
            pe.wait_ge(low_sum_ok, WCH)
            pe.wait_ge(consts_ok, 3)
            nc.tensor.matmul(bank[2][0:1, 0:WCH], ones[:], low_sum[:], start=True, stop=True).then_inc(low_all, 1)
            turn_probs(STEPS - 3)
            pe.wait_ge(low_flag_ok, 1)
            has_low = pe.value_load(low_flag[0:1, 0:1], min_val=0, max_val=2**31 - 1)

            def rest(low):

                def ffn_product(dst, lhs, rhs, first, last):
                    (ar, al), (br, bl) = lhs, rhs
                    nc.tensor.matmul(dst, ar, br, start=first, stop=False)
                    if low:
                        nc.tensor.matmul(dst, al, br, start=False, stop=False)
                    return nc.tensor.matmul(dst, ar, bl, start=False, stop=last)

                def gated(t, c):
                    feats = slice(P * c, P * (c + 1))
                    cols = bass.ts(t, TILE)
                    pe.wait_ge(u_ok, HC * t + c + BUFS)
                    ffn_product(gate_ps, (wf_r[:, W1, feats], wf_l[:, W1, feats]),
                                (xt_r[:, cols], xt_l[:, cols]), True, True).then_inc(gate_done, 1)
                    pe.wait_ge(h0_ok, HC * t + c + 1)
                    ffn_product(up_ps, (wf_r[:, W2, feats], wf_l[:, W2, feats]),
                                (xt_r[:, cols], xt_l[:, cols]), True, True).then_inc(up_done, 1)

                def hidden1(t, c):
                    pe.wait_ge(h1f_ok, HC * t + c + 1)
                    for k in range(HC):
                        if c == 0:
                            pe.wait_ge(h0l_dve if k % 2 else h0l_pool, 2 * t + k // 2 + 2)
                        last = ffn_product(h1_ps[c % 2], (wf_r[:, H1 + k, P * c:P * (c + 1)], wf_l[:, H1 + k, P * c:P * (c + 1)]),
                                           (h0_r[:, k, :], h0_l[:, k, :]), k == 0, k == HC - 1)
                    last.then_inc(h1_done, 1)

                def hidden2(t, c):
                    pe.wait_ge(h2f_ok, HC * t + c + 1)
                    for k in range(HC):
                        if c == 0:
                            pe.wait_ge(h1l_ok, HC * t + k + 1 + BUFS)
                        last = ffn_product(h2_ps[c % 2], (wf_r[:, H2 + k, P * c:P * (c + 1)], wf_l[:, H2 + k, P * c:P * (c + 1)]),
                                           (h1_r[:, k, :], h1_l[:, k, :]), k == 0, k == HC - 1)
                    last.then_inc(h2_done, 1)

                def project(t):
                    pe.wait_ge(yT_ok, t + 1)
                    for k in range(HC):
                        pe.wait_ge(h2l_ok, HC * t + k + 1 + BUFS)
                        last = ffn_product(y_ps, (wf_r[:, W3, P * k:P * (k + 1)], wf_l[:, W3, P * k:P * (k + 1)]),
                                           (h2_r[:, k, :], h2_l[:, k, :]), k == 0, k == HC - 1)
                    last.then_inc(y_done, 1)

                def turn_y(t):
                    pe.wait_ge(yT_ok, t + 2)
                    pe.wait_ge(z_ok, t + 1)
                    for j in range(4):
                        last = nc.tensor.transpose(yn_ps[:, D * j:D * (j + 1)], yT[:, P * j:P * (j + 1)], ident[:])
                    last.then_inc(yn_done, 1)

                pe.wait_ge(x1Tl_ok, 2)
                scores(STEPS - 1)
                turn_x1(PAIRS - 5)
                weigh_values(PAIRS - 3, 1)
                pe.wait_ge(exp_ok, STEPS - 1)
                gated(0, 0)
                turn_probs(STEPS - 2)
                turn_back(PAIRS - 3)
                gated(0, 1)
                weigh_values(PAIRS - 2, 0)
                turn_probs(STEPS - 1)
                gated(0, 2)
                weigh_values(PAIRS - 2, 1)
                turn_x1(PAIRS - 4)
                gated(0, 3)
                turn_back(PAIRS - 2)
                weigh_values(PAIRS - 1, 0)
                weigh_values(PAIRS - 1, 1)

                hidden1(0, 0)

                def tile(t, first=False, last=False):
                    if first:
                        turn_x1(PAIRS - 3)
                        turn_back(PAIRS - 1)
                    if not last:
                        gated(t + 1, 0)
                    if not first:
                        project(t - 1)
                    hidden1(t, 1)
                    if first:
                        turn_x1(PAIRS - 2)
                    else:
                        turn_y(t - 1)
                    if not last:
                        gated(t + 1, 1)
                    hidden1(t, 2)
                    hidden1(t, 3)
                    if not last:
                        gated(t + 1, 2)
                    if first:
                        turn_x1(PAIRS - 1)
                    hidden2(t, 0)
                    if first:
                        pe.wait_ge(x1Tl_ok, PAIRS - 1)
                    hidden2(t, 1)
                    if not last:
                        gated(t + 1, 3)
                    hidden2(t, 2)
                    hidden2(t, 3)
                    if first:
                        pe.wait_ge(x1Tl_ok, PAIRS)
                    if not last:
                        hidden1(t + 1, 0)

                tile(0, first=True)
                with pe.Fori(1, NT - 1) as t:
                    tile(t)
                tile(NT - 1, last=True)
                project(NT - 1)
                turn_y(NT - 1)

            with pe.If(has_low != 0):
                rest(True)
            with pe.Else():
                rest(False)

        @block.scalar
        def _(act):
            for s in (h1f_ok, h2f_ok):
                act.sem_inc(s, BUFS)
            act.sem_inc(yT_ok, 1)

            for t in range(NT):
                act.wait_ge(xT_in[t], 16)
                nc.scalar.copy(xt_r[:, TILE * t:TILE * (t + 1)], xt32[:, TILE * t:TILE * (t + 1)]).then_inc(xT_r, 1)
            act.wait_ge(small_in, 32)
            act.wait_ge(bqs_ok, 1)
            for t in range(NT):
                cols = slice(TILE * t, TILE * (t + 1))
                act.wait_ge(k_done, t + 1)
                nc.scalar.activation(k_r[:, cols], bank[t], ACT.Identity, bias=vec[:, BK:BK + 1]).then_inc(kr_ok, 1)
                act.wait_ge(q_done, t + 1)
                nc.scalar.activation(q32[:, cols], bank[4 + t], ACT.Identity, bias=bqs[:], scale=SCALE).then_inc(q32_ok, 1)

            def soften(s):
                act.wait_ge(max_ok, s + 1)
                if s >= 2:
                    act.wait_ge(pt_done, 2 * s - 2)
                nc.scalar.activation(probs[:, s % 2, :], score[s % 2], ACT.Exp, bias=negmax[:, s:s + 1],
                                     accum_out=rowsum[:, s:s + 1]).then_inc(exp_ok, 1)

            def round_v(t):
                act.wait_ge(v32_ok, t + 1)
                nc.scalar.copy(v_r[:, 4 * t:4 * t + 4, :], xt32[:, TILE * t:TILE * (t + 1)].rearrange("p (n d) -> p n d", d=D)).then_inc(vr_ok, 1)

            def round_probs(s, h):
                p = s // 2
                act.wait_ge(pt_done, 2 * s + h + 1)
                if p >= 2:
                    act.wait_ge(pv_done, p - 1)
                nc.scalar.copy(pt_r[:, p % 2, 4 * h:4 * h + 4, P * (s % 2):P * (s % 2) + P],
                               pt_ps[h].rearrange("p (k q) -> p k q", q=P)).then_inc(ptr_ok, 1)

            def sum_low(n):
                act.wait_ge(wfl_ok, n + 1)
                if n:
                    act.wait_ge(low_sum_ok, n)
                nc.scalar.activation(low_abs[:], wf_l[:, n, :].bitcast(F32), ACT.Abs, scale=2.0 ** 64,
                                     accum_out=low_sum[:, n:n + 1]).then_inc(low_sum_ok, 1)

            def take_oT(p):
                act.wait_ge(pv_done, p + 1)
                if p >= 2:
                    act.wait_ge(back_done, p - 1)
                nc.scalar.copy(oT[:, p % 2, :], pv_ps[:, 0:256]).then_inc(oT_ok, 1)

            def divide(p):
                act.wait_ge(back_done, p + 1)
                act.wait_ge(rinv_ok, p + 1)
                if p >= 2:
                    act.wait_ge(resid_ok, p - 1)
                for u in range(2):
                    last = nc.scalar.activation(attn[:, p % 2, u, :], misc_ps[:, D * u:D * (u + 1)], ACT.Identity,
                                                scale=rinv[:, 2 * p + u:2 * p + u + 1])
                last.then_inc(attn_ok, 1)

            def round_x1(p):
                act.wait_ge(x1T_done, p + 1)
                nc.scalar.copy(xt_r[:, 256 * p:256 * (p + 1)], x1T_ps[p][:, 0:256]).then_inc(x1Tr_ok, 1)

            def tanh_gate(t, c):
                act.wait_ge(gate_done, HC * t + c + 1)
                act.wait_ge(u_ok, HC * t + c + 1)
                nc.scalar.activation(tanh_g[:, c % 2, :], gate_ps, ACT.Tanh, scale=half_s1[:, c:c + 1]).then_inc(tanh_ok, 1)

            def round_h0(t, c):
                act.wait_ge(h0_ok, HC * t + c + 2)
                nc.scalar.copy(h0_r[:, c, :], h0_32[:, c % 2, :]).then_inc(h0r_ok, 1)

            soften(0)
            round_v(0)
            round_v(1)
            for s in range(STEPS + 2):
                if s >= 4 and s % 2 == 0:
                    take_oT((s - 4) // 2)
                if s >= 5 and s % 2 == 1:
                    divide((s - 5) // 2)
                if s >= 8 and s % 2 == 0:
                    round_x1((s - 8) // 2)
                if s == STEPS - 2:
                    act.wait_ge(half_s_ok, 2)
                    tanh_gate(0, 0)
                if s < STEPS:
                    round_probs(s, 0)
                    round_probs(s, 1)
                if s + 1 < STEPS:
                    soften(s + 1)
                if s == 0:
                    round_v(2)
                    round_v(3)
                if 2 <= s < 2 + WCH:
                    sum_low(s - 2)
                if STEPS - 2 <= s <= STEPS:
                    tanh_gate(0, s - (STEPS - 3))
                    round_h0(0, s - (STEPS - 2))
            round_h0(0, 3)
            take_oT(PAIRS - 1)
            nc.scalar.preload_act_table(ACT.Gelu)
            round_x1(PAIRS - 3)

            def gelu(t, c, psum, done, value, scale, dst_r, r_ok, f_ok, l_ok, slot):
                act.wait_ge(done, value)
                nc.scalar.activation(dst_r[:, c, :], psum[c % 2], ACT.Gelu, scale=vec[:, scale + c:scale + c + 1]).then_inc(r_ok, 1)
                act.wait_ge(l_ok, HC * t + c + 1)
                nc.scalar.activation(h32[:, slot + c % 2, :], psum[c % 2], ACT.Gelu, scale=vec[:, scale + c:scale + c + 1]).then_inc(f_ok, 1)

            def gelu1(t, c):
                if c == 0:
                    act.wait_ge(h2_done, HC * t + 1)
                gelu(t, c, h1_ps, h1_done, HC * t + c + 1, HS1, h1_r, h1r_ok, h1f_ok, h1l_ok, 0)

            def gelu2(t, c):
                if c == 0:
                    act.wait_ge(y_done, t + 1)
                gelu(t, c, h2_ps, h2_done, HC * t + c + 2, HS2, h2_r, h2r_ok, h2f_ok, h2l_ok, 2)

            def take_y(t):
                act.wait_ge(y_done, t + 2)
                act.wait_ge(yn_done, t + 1)
                nc.scalar.activation(yT, y_ps, ACT.Identity, scale=vec[:, S3:S3 + 1]).then_inc(yT_ok, 1)

            gelu1(0, 0)

            def tile(t, first=False, last=False):
                if first:
                    divide(PAIRS - 1)
                if not last:
                    tanh_gate(t + 1, 0)
                if not first:
                    take_y(t - 1)
                gelu1(t, 1)
                if first:
                    round_x1(PAIRS - 2)
                if not last:
                    tanh_gate(t + 1, 1)
                gelu1(t, 2)
                gelu1(t, 3)
                if not last:
                    round_h0(t + 1, 0)
                    tanh_gate(t + 1, 2)
                    round_h0(t + 1, 1)
                if first:
                    round_x1(PAIRS - 1)
                gelu2(t, 0)
                gelu2(t, 1)
                if not last:
                    round_h0(t + 1, 2)
                    tanh_gate(t + 1, 3)
                gelu2(t, 2)
                if not last:
                    round_h0(t + 1, 3)
                gelu2(t, 3)
                if not last:
                    gelu1(t + 1, 0)

            tile(0, first=True)
            with act.Fori(1, NT - 1) as t:
                tile(t)
            tile(NT - 1, last=True)
            take_y(NT - 1)

        @block.vector
        def _(dve):
            for s in (u_ok, h1l_ok, h2l_ok):
                dve.sem_inc(s, BUFS)
            for s in (h0_ok, h0l_dve, z_ok):
                dve.sem_inc(s, 1)

            dve.wait_ge(wqkv_in, 16)
            nc.vector.tensor_copy(w_r, w32[:]).then_inc(wqkv_r, 1)
            dve.wait_ge(wqkv_r, 1)
            nc.vector.tensor_tensor(w_l, w32[:], w_r.bitcast(F32), ALU.subtract).then_inc(wqkv_l, 1)

            def split_xT(t):
                cols = slice(TILE * t, TILE * (t + 1))
                dve.wait_ge(xT_r, t + 1)
                nc.vector.tensor_tensor(xt_l[:, cols], xt32[:, cols], xt_r[:, cols].bitcast(F32), ALU.subtract).then_inc(xT_l, 1)

            def split_k(t):
                cols = slice(TILE * t, TILE * (t + 1))
                dve.wait_ge(kr_ok, t + 1)
                nc.vector.scalar_tensor_tensor(out=k_l[:, cols], in0=bank[t], scalar=vec[:, BK:BK + 1],
                                               in1=k_r[:, cols].bitcast(F32), op0=ALU.add, op1=ALU.subtract).then_inc(kl_ok, 1)

            split_xT(0)
            dve.wait_ge(small_in, 32)
            nc.vector.tensor_scalar(bqs[:], vec[:, BQ:BQ + 1], SCALE, None, ALU.mult).then_inc(bqs_ok, 1)
            for t in range(1, NT):
                split_xT(t)
            for t in range(NT):
                split_k(t)
            nc.vector.tensor_scalar(half_s1[:], vec[:, S1:S1 + HC], 0.5, None, ALU.mult).then_inc(half_s_ok, 1)
            dve.wait_ge(half_s_ok, 1)
            nc.vector.tensor_tensor(half_s1s2[:], half_s1[:], vec[:, S2:S2 + HC], ALU.mult).then_inc(half_s_ok, 1)

            def row_max(s):
                dve.wait_ge(s_done, s + 1)
                nc.vector.tensor_reduce(negmax[:, s:s + 1], score[s % 2], AX.X, ALU.max, negate=True).then_inc(max_ok, 1)

            def bias_v(t):
                dve.wait_ge(v_done, t + 1)
                dst = xt32[:, TILE * t:TILE * (t + 1)].rearrange("p (n d) -> p n d", d=D)
                src = bank[4 + t].rearrange("p (n d) -> p n d", d=D)
                nc.vector.tensor_tensor(dst, src, bvb[:].unsqueeze(1).broadcast_to([P, 4, D]), ALU.add).then_inc(v32_ok, 1)

            def split_probs(s, h):
                p = s // 2
                dve.wait_ge(ptr_ok, 2 * s + h + 1)
                q = slice(P * (s % 2), P * (s % 2) + P)
                nc.vector.tensor_tensor(pt_l[:, p % 2, 4 * h:4 * h + 4, q], pt_ps[h].rearrange("p (k q) -> p k q", q=P),
                                        pt_r[:, p % 2, 4 * h:4 * h + 4, q].bitcast(F32), ALU.subtract).then_inc(ptl_ok, 1)

            def invert_sums(p):
                dve.wait_ge(exp_ok, 2 * p + 2)
                nc.vector.reciprocal(rinv[:, 2 * p:2 * p + 2], rowsum[:, 2 * p:2 * p + 2]).then_inc(rinv_ok, 1)

            def stats1(p):
                dve.wait_ge(resid_ok, p + 1)
                if p:
                    dve.wait_ge(mv1_ok, p)
                for u in range(2):
                    nc.vector.bn_stats(bn6[:, u, :], xn[:, 2 * p + u, :]).then_inc(bn1_ok, 1)
                for u in range(2):
                    dve.wait_ge(bn1_ok, 2 * p + u + 1)
                    last = nc.vector.bn_aggr(mv1[:, 2 * p + u, :], bn6[:, u, :])
                last.then_inc(mv1_ok, 1)

            def normalise1(p):
                dve.wait_ge(rstd1_ok, p + 1)
                for s in (2 * p, 2 * p + 1):
                    last = nc.vector.tensor_scalar(xn[:, s, :], xn[:, s, :], mv1[:, s, 0:1], rstd1[:, s:s + 1], ALU.subtract, ALU.mult)
                last.then_inc(x1_ok, 1)

            def split_x1(p):
                dve.wait_ge(x1Tr_ok, p + 1)
                nc.vector.tensor_tensor(xt_l[:, 256 * p:256 * (p + 1)], x1T_ps[p][:, 0:256],
                                        xt_r[:, 256 * p:256 * (p + 1)].bitcast(F32), ALU.subtract).then_inc(x1Tl_ok, 1)

            def round_weights(n):
                dve.wait_ge(raw_in[n % RAW_SLOTS], 16 * (n // RAW_SLOTS + 1))
                nc.vector.tensor_copy(wf_r[:, n, :], raw[:, n % RAW_SLOTS, :]).then_inc(wfr_ok, 1)

            def gate_u(t, c):
                dve.wait_ge(tanh_ok, HC * t + c + 1)
                nc.vector.scalar_tensor_tensor(out=u32[:, c % 2, :], in0=tanh_g[:, c % 2, :], scalar=1.0,
                                               in1=gate_ps, op0=ALU.add, op1=ALU.mult).then_inc(u_ok, 1)

            def gate_h0(t, c):
                dve.wait_ge(u_ok, HC * t + c + 1 + BUFS)
                dve.wait_ge(up_done, HC * t + c + 1)
                dve.wait_ge(h0l_dve if c % 2 else h0l_pool, 2 * t + c // 2 + 1)
                nc.vector.scalar_tensor_tensor(out=h0_32[:, c % 2, :], in0=up_ps, scalar=half_s1s2[:, c:c + 1],
                                               in1=u32[:, c % 2, :], op0=ALU.mult, op1=ALU.mult).then_inc(h0_ok, 1)

            def gate(t, c):
                gate_u(t, c)
                gate_h0(t, c)

            def split_h0(t, c):
                dve.wait_ge(h0r_ok, HC * t + c + 1)
                nc.vector.tensor_tensor(h0_l[:, c, :], h0_32[:, c % 2, :], h0_r[:, c, :].bitcast(F32), ALU.subtract).then_inc(h0l_dve, 1)

            row_max(0)
            bias_v(0)
            bias_v(1)
            row_max(1)
            bias_v(2)
            bias_v(3)
            for s in range(STEPS + 2):
                if s >= 8 and s % 2 == 0:
                    split_x1((s - 8) // 2)
                if s == STEPS - 2:
                    dve.wait_ge(half_s_ok, 2)
                    gate(0, 0)
                if s == STEPS - 3:
                    dve.wait_ge(low_all, 1)
                    nc.vector.tensor_reduce(low_flag[:].bitcast(F32), bank[2][0:1, 0:WCH], AX.X, ALU.add).then_inc(low_flag_ok, 1)
                if s < STEPS:
                    split_probs(s, 0)
                    split_probs(s, 1)
                if s + 2 < STEPS:
                    row_max(s + 2)
                if s % 2 == 1 and s < STEPS:
                    invert_sums(s // 2)
                if s >= 6 and s % 2 == 0 and s < STEPS:
                    stats1((s - 6) // 2)
                if s < WCH:
                    round_weights(s)
                if s == STEPS - 2:
                    gate(0, 1)
                if s == STEPS - 1:
                    gate(0, 2)
                    split_h0(0, 1)
                if s == STEPS:
                    gate(0, 3)
                    stats1(PAIRS - 3)
                if s == STEPS + 1:
                    split_h0(0, 3)
                    stats1(PAIRS - 2)
            split_x1(PAIRS - 3)
            normalise1(PAIRS - 2)

            def split_h(t, c, f_ok, slot, dst_r, dst_l, l_ok):
                dve.wait_ge(f_ok, HC * t + c + 1 + BUFS)
                nc.vector.tensor_tensor(dst_l[:, c, :], h32[:, slot + c % 2, :], dst_r[:, c, :].bitcast(F32), ALU.subtract).then_inc(l_ok, 1)

            def split_h1(t, c):
                split_h(t, c, h1f_ok, 0, h1_r, h1_l, h1l_ok)

            def split_h2(t, c):
                split_h(t, c, h2f_ok, 2, h2_r, h2_l, h2l_ok)

            def add_residual2(t):
                dve.wait_ge(yn_done, t + 2)
                dve.wait_ge(out_stored, 16 * t + 16)
                nc.vector.tensor_tensor(z, yn_ps.rearrange("p (j d) -> p j d", d=D),
                                        xn[:, bass.ts(t, 4), :], ALU.add).then_inc(z_ok, 1)

            def stats2(t):
                dve.wait_ge(z_ok, t + 2)
                for j in range(4):
                    last = nc.vector.bn_stats(bn6[:, j, :], z[:, j, :])
                dve.drain()
                for j in range(4):
                    last = nc.vector.bn_aggr(mv2[:, j, :], bn6[:, j, :])
                last.then_inc(mv2_ok, 1)

            def normalise2(t):
                dve.wait_ge(rstd2_ok, t + 1)
                for j in range(4):
                    last = nc.vector.tensor_scalar(z[:, j, :], z[:, j, :], mv2[:, j, 0:1], rstd2[:, j:j + 1], ALU.subtract, ALU.mult)
                last.then_inc(out_ok, 1)

            split_h1(0, 0)

            def tile(t, first=False, last=False):
                if not last:
                    gate(t + 1, 0)
                if first:
                    stats1(PAIRS - 1)
                else:
                    add_residual2(t - 1)
                split_h1(t, 1)
                if first:
                    split_x1(PAIRS - 2)
                if not last:
                    gate(t + 1, 1)
                if first:
                    normalise1(PAIRS - 1)
                else:
                    stats2(t - 1)
                split_h1(t, 2)
                split_h1(t, 3)
                if not last:
                    gate_u(t + 1, 2)
                    split_h0(t + 1, 1)
                    gate_h0(t + 1, 2)
                if first:
                    split_x1(PAIRS - 1)
                else:
                    normalise2(t - 1)
                split_h2(t, 0)
                split_h2(t, 1)
                if not last:
                    gate(t + 1, 3)
                split_h2(t, 2)
                if not last:
                    split_h0(t + 1, 3)
                split_h2(t, 3)
                if not last:
                    split_h1(t + 1, 0)

            tile(0, first=True)
            with dve.Fori(1, NT - 1) as t:
                tile(t)
            tile(NT - 1, last=True)
            add_residual2(NT - 1)
            stats2(NT - 1)
            normalise2(NT - 1)

        @block.gpsimd
        def _(pool):
            pool.sem_inc(h0l_pool, 1)
            nc.gpsimd.memset(mhalf[:], -0.5).then_inc(consts_ok, 1)
            nc.gpsimd.memset(eps[:], EPS).then_inc(consts_ok, 1)
            nc.gpsimd.memset(ones[:], 1.0).then_inc(consts_ok, 1)

            def split_q(p):
                i, b = p // 2, p % 2
                src = q32[:, S * b + 256 * i:S * b + 256 * (i + 1)]
                if p < 4:
                    pool.wait_ge(q32_ok, 2 * b + i // 2 + 1)
                if p >= 2:
                    pool.wait_ge(s_done, 2 * p - 2)
                nc.gpsimd.tensor_copy(q_r[:, p % 2, :], src).then_inc(qr_ok, 1)
                pool.wait_ge(qr_ok, p + 1)
                nc.gpsimd.tensor_tensor(q_l[:, p % 2, :], src, q_r[:, p % 2, :].bitcast(F32), ALU.subtract).then_inc(ql_ok, 1)

            def split_v(t):
                pool.wait_ge(vr_ok, t + 1)
                src = xt32[:, TILE * t:TILE * (t + 1)].rearrange("p (n d) -> p n d", d=D)
                nc.gpsimd.tensor_tensor(v_l[:, 4 * t:4 * t + 4, :], src, v_r[:, 4 * t:4 * t + 4, :].bitcast(F32), ALU.subtract).then_inc(vl_ok, 1)

            def add_residual(p):
                pool.wait_ge(attn_ok, p + 1)
                if p == 0:
                    pool.wait_ge(x_in, 16)
                nc.gpsimd.tensor_tensor(xn[:, 2 * p:2 * p + 2, :], attn[:, p % 2, :, :], xn[:, 2 * p:2 * p + 2, :], ALU.add).then_inc(resid_ok, 1)

            def normalise1(p):
                two = slice(2 * p, 2 * p + 2)
                pool.wait_ge(mv1_ok, p + 1)
                nc.gpsimd.tensor_scalar(rstd1[:, two], mv1[:, two, 1], EPS, None, ALU.add).then_inc(var1_ok, 1)
                pool.wait_ge(var1_ok, p + 1)
                pool.wait_ge(consts_ok, 3)
                nc.gpsimd.tensor_tensor(rstd1[:, two], rstd1[:, two], mhalf[:, 0:2], ALU.pow).then_inc(rstd1_ok, 1)
                if p < PAIRS - 2:
                    nc.gpsimd.tensor_tensor(xn[:, two, :], xn[:, two, :], mv1[:, two, 0:1].broadcast_to([P, 2, D]), ALU.subtract).then_inc(centre1_ok, 1)
                    pool.wait_ge(rstd1_ok, p + 1)
                    pool.wait_ge(centre1_ok, p + 1)
                    nc.gpsimd.tensor_tensor(xn[:, two, :], xn[:, two, :], rstd1[:, two].unsqueeze(2).broadcast_to([P, 2, D]), ALU.mult).then_inc(x1_ok, 1)

            def split_weights(n):
                pool.wait_ge(wfr_ok, n + 1)
                nc.gpsimd.tensor_tensor(wf_l[:, n, :], raw[:, n % RAW_SLOTS, :], wf_r[:, n, :].bitcast(F32), ALU.subtract).then_inc(wfl_ok, 1)

            def split_h0(t, c):
                pool.wait_ge(h0r_ok, HC * t + c + 1)
                nc.gpsimd.tensor_tensor(h0_l[:, c, :], h0_32[:, c % 2, :], h0_r[:, c, :].bitcast(F32), ALU.subtract).then_inc(h0l_pool, 1)

            split_q(0)
            split_q(1)
            for t in range(NT):
                split_v(t)
            for s in range(STEPS + 2):
                if s % 2 == 0 and s // 2 + 2 < PAIRS:
                    split_q(s // 2 + 2)
                if s >= 5 and s % 2 == 1 and s < STEPS:
                    add_residual((s - 5) // 2)
                if s == STEPS:
                    split_h0(0, 2)
                    add_residual(PAIRS - 2)
                if s >= 6 and s % 2 == 0:
                    normalise1((s - 6) // 2)
                if s < WCH:
                    split_weights(s)
                if s == STEPS - 2:
                    split_h0(0, 0)
            normalise1(PAIRS - 2)
            add_residual(PAIRS - 1)
            normalise1(PAIRS - 1)

            def invert_std2(t):
                pool.wait_ge(mv2_ok, t + 1)
                nc.gpsimd.tensor_tensor(rstd2[:], mv2[:, :, 1], eps[:], ALU.add).then_inc(var2_ok, 1)
                pool.wait_ge(var2_ok, t + 1)
                nc.gpsimd.tensor_tensor(rstd2[:], rstd2[:], mhalf[:], ALU.pow).then_inc(rstd2_ok, 1)

            def tile(t, first=False):
                if not first:
                    invert_std2(t - 1)
                split_h0(t + 1, 0)
                split_h0(t + 1, 2)

            tile(0, first=True)
            with pool.Fori(1, NT - 1) as t:
                tile(t)
            for t in (NT - 2, NT - 1):
                invert_std2(t)


def kernel(L0_attn_X, L0_attn_W_q, L0_attn_W_k, L0_attn_W_v, L0_attn_b_q, L0_attn_b_k, L0_attn_b_v,
           L0_ffn_w1_w, L0_ffn_w1_s, L0_ffn_w2_w, L0_ffn_w2_s, L0_ffn_h1_w, L0_ffn_h1_s,
           L0_ffn_h2_w, L0_ffn_h2_s, L0_ffn_w3_w, L0_ffn_w3_s):
    import numpy as np
    import concourse.bacc as bacc
    from concourse.bass_utils import run_bass_kernel_spmd

    def chunked(w):
        wt = np.asarray(w).T
        return wt.reshape(-1, P, wt.shape[1]).transpose(1, 0, 2)

    def column(v):
        return np.asarray(v).reshape(-1, P).T

    x = np.ascontiguousarray(L0_attn_X)
    arrays = {
        "x": np.ascontiguousarray(x.reshape(B, NT, 2, P, D).transpose(3, 1, 0, 2, 4)).reshape(P, STEPS, D),
        "xT": np.ascontiguousarray(x.reshape(B * S, D).T),
        "wqkv": np.ascontiguousarray(np.stack([L0_attn_W_q, L0_attn_W_k, L0_attn_W_v], axis=1)),
        "bv": np.ascontiguousarray(L0_attn_b_v).reshape(1, D),
        "vecs": np.ascontiguousarray(np.concatenate([column(v) for v in (
            L0_attn_b_q, L0_attn_b_k, L0_ffn_w1_s, L0_ffn_w2_s, L0_ffn_h1_s, L0_ffn_h2_s, L0_ffn_w3_s)], axis=1)),
        "wffn": np.ascontiguousarray(np.concatenate(
            [chunked(L0_ffn_w1_w), chunked(L0_ffn_w2_w), chunked(L0_ffn_w3_w).reshape(P, 1, HID),
             chunked(L0_ffn_h1_w), chunked(L0_ffn_h2_w)], axis=1)),
        "eye": np.eye(P, dtype=np.float32),
    }
    nc = bacc.Bacc("TRN2", target_bir_lowering=False, num_devices=1)
    args = [nc.dram_tensor(n, arrays[n].shape, mybir.dt.from_np(arrays[n].dtype), kind="ExternalInput").ap()
            for n in ("xT", "x", "wqkv", "bv", "vecs", "wffn", "eye")]
    args.append(nc.dram_tensor("out", (P, STEPS, D), F32, kind="ExternalOutput").ap())
    build(nc, *args)
    r = run_bass_kernel_spmd(nc, [arrays], core_ids=[0])
    by_step = r.results[0]["out"].reshape(P, NT, B, 2, D)
    return np.ascontiguousarray(by_step.transpose(2, 1, 3, 0, 4)).reshape(B, S, D)
```

```python
from contextlib import ExitStack

import concourse.bass as bass
from concourse import mybir

F32 = mybir.dt.float32
F32R = mybir.dt.float32r
ALU = mybir.AluOpType
ACT = mybir.ActivationFunctionType
AX = mybir.AxisListType

P = 128
B, S, D = 2, 1024, 128
HID = 512
TILE = 512
NT = B * S // TILE
LAST = NT - 1
HALF = TILE // 2
STEPS = B * S // P
PAIRS = STEPS // 2
KB = S // P
HC = HID // P
SCALE = D ** -0.5
EPS = 1e-5

W1, W2, W3, H1, H2 = 0, 1, 2, 3, 3 + HC
WCH = H2 + HC
RAW_SLOTS = 4

BUFS = 2

BQ, BK, S1, S2, HS1, HS2, S3 = 0, 1, 2, 2 + HC, 2 + 2 * HC, 2 + 3 * HC, 2 + 4 * HC
VECS = S3 + 1


def build(nc, xT, x, wqkv, bv, vecs, wffn, eye, out):
    with ExitStack() as ctx:
        def sb(name, shape, dt):
            return ctx.enter_context(nc.sbuf_tensor(name, shape, dt))

        def ps(name, shape):
            return ctx.enter_context(nc.psum_tensor(name, shape, F32))

        def sem(name):
            return ctx.enter_context(nc.semaphore(name))

        arena_a = sb("arena_a", [P, 16384], F32R)
        arena_b = sb("arena_b", [P, 5888], F32R)
        arena_c = sb("arena_c", [P, 6144], F32)
        pt_r = arena_a[:, 0:4096].rearrange("p (a k q) -> p a k q", a=2, k=KB)
        pt_l = arena_a[:, 4096:8192].rearrange("p (a k q) -> p a k q", a=2, k=KB)
        k_r = arena_a[:, 8192:10240]
        k_l = arena_a[:, 10240:12288]
        v_r = arena_a[:, 12288:14336].rearrange("p (n d) -> p n d", d=D)
        v_l = arena_a[:, 14336:16384].rearrange("p (n d) -> p n d", d=D)
        h1_r = arena_a[:, 0:2048].rearrange("p (c n) -> p c n", c=HC)
        h1_l = arena_a[:, 2048:4096].rearrange("p (c n) -> p c n", c=HC)
        h2_r = arena_a[:, 4096:6144].rearrange("p (c n) -> p c n", c=HC)
        h2_l = arena_a[:, 6144:8192].rearrange("p (c n) -> p c n", c=HC)
        xt_r = arena_b[:, 0:2048]
        xt_l = arena_b[:, 2048:4096]
        q_r = arena_b[:, 4096:4608].rearrange("p (a q) -> p a q", a=2)
        q_l = arena_b[:, 4608:5120].rearrange("p (a q) -> p a q", a=2)
        w_r = arena_b[:, 5120:5504].rearrange("p (w d) -> p w d", w=3)
        w_l = arena_b[:, 5504:5888].rearrange("p (w d) -> p w d", w=3)
        xt32 = arena_c[:, 0:2048]
        q32 = arena_c[:, 2048:4096]
        probs = arena_c[:, 4096:6144].rearrange("p (a k) -> p a k", a=2)
        tanh_g = arena_c[:, 0:1024].rearrange("p (a n) -> p a n", a=BUFS)
        u32 = arena_c[:, 1024:2048].rearrange("p (a n) -> p a n", a=BUFS)
        h0_32 = arena_c[:, 2048:3072].rearrange("p (a n) -> p a n", a=BUFS)
        yT = arena_c[:, 3072:3584]
        z = arena_c[:, 3584:4096].rearrange("p (j d) -> p j d", d=D)
        h32 = arena_c[:, 4096:6144].rearrange("p (a n) -> p a n", a=2 * BUFS)
        z_end = sb("z_end", [P, 4, D], F32)
        h0_r = sb("h0_r", [P, HC, TILE], F32R)
        h0_l = sb("h0_l", [P, HC, TILE], F32R)

        xn = sb("xn", [P, STEPS, D], F32)
        oT = sb("oT", [P, 2, 256], F32)
        attn = sb("attn", [P, 2, 2, D], F32)
        raw = sb("raw", [P, RAW_SLOTS, 512], F32)
        wf_r = sb("wf_r", [P, WCH, 512], F32R)
        wf_l = sb("wf_l", [P, WCH, 512], F32R)
        w32 = sb("w32", [P, 3, D], F32)
        bvb = sb("bvb", [P, D], F32)
        vec = sb("vec", [P, VECS], F32)
        bqs = sb("bqs", [P, 1], F32)
        half_s1 = sb("half_s1", [P, HC], F32)
        half_s1s2 = sb("half_s1s2", [P, HC], F32)
        ident = sb("ident", [P, P], F32)
        negmax = sb("negmax", [P, STEPS], F32)
        rowsum = sb("rowsum", [P, STEPS], F32)
        rinv = sb("rinv", [P, STEPS], F32)
        bn6 = sb("bn6", [P, 4, 6], F32)
        mv1 = sb("mv1", [P, STEPS, 2], F32)
        rstd1 = sb("rstd1", [P, STEPS], F32)
        mv2 = sb("mv2", [P, 4, 2], F32)
        rstd2 = sb("rstd2", [P, 4], F32)
        low_abs = sb("low_abs", [P, 512], F32)
        low_sum = sb("low_sum", [P, WCH], F32)
        low_flag = sb("low_flag", [1, 1], mybir.dt.int32)
        ones = sb("ones", [P, 1], F32)
        mhalf = sb("mhalf", [P, 4], F32)
        eps = sb("eps", [P, 4], F32)

        psum = ps("psum", [P, 8 * TILE])
        bank = [psum[:, TILE * i:TILE * (i + 1)] for i in range(8)]
        score = [psum[:, 2 * TILE * i:2 * TILE * (i + 1)] for i in range(2)]
        pt_ps = [bank[4], bank[5]]
        pv_ps, misc_ps = bank[6], bank[7]
        gate_ps, up_ps = bank[0], bank[1]
        h2_ps, h1_ps = [bank[2], bank[3]], [bank[4], bank[5]]
        y_ps, yn_ps = bank[6], bank[7]
        h2_end = [bank[2], bank[3], bank[1]]
        y_end, yn_end = [bank[6], bank[0]], [bank[7], bank[4]]
        x1T_ps = [misc_ps] * (PAIRS - 3) + [bank[3], bank[2], misc_ps]

        WARM_UPS = 8

        xT_in = [sem(f"xT_in{t}") for t in range(NT)]
        wqkv_in, small_in, x_in, eye_in, out_stored = (
            sem("wqkv_in"), sem("small_in"), sem("x_in"), sem("eye_in"), sem("out_stored"))
        raw_in = [sem(f"raw_in{n}") for n in range(RAW_SLOTS)]
        warm_ok = sem("warm_ok")
        wqkv_r, wqkv_l, bqs_ok = sem("wqkv_r"), sem("wqkv_l"), sem("bqs_ok")
        xT_r, xT_l = sem("xT_r"), sem("xT_l")
        k_done, q_done, v_done = sem("k_done"), sem("q_done"), sem("v_done")
        kr_ok, kl_ok, q32_ok = sem("kr_ok"), sem("kl_ok"), sem("q32_ok")
        v32_ok, vr_ok, vl_ok = sem("v32_ok"), sem("vr_ok"), sem("vl_ok")
        qr_ok, ql_ok = sem("qr_ok"), sem("ql_ok")
        s_done, max_ok, exp_ok, rinv_ok = sem("s_done"), sem("max_ok"), sem("exp_ok"), sem("rinv_ok")
        pt_done, ptr_ok, ptl_ok = sem("pt_done"), sem("ptr_ok"), sem("ptl_ok")
        pv_done, oT_ok, back_done, attn_ok = sem("pv_done"), sem("oT_ok"), sem("back_done"), sem("attn_ok")
        resid_ok, bn1_ok, mv1_ok = sem("resid_ok"), sem("bn1_ok"), sem("mv1_ok")
        var1_ok, rstd1_ok, centre1_ok, x1_ok = sem("var1_ok"), sem("rstd1_ok"), sem("centre1_ok"), sem("x1_ok")
        x1T_done, x1Tr_ok, x1Tl_ok = sem("x1T_done"), sem("x1Tr_ok"), sem("x1Tl_ok")
        wfr_ok, wfl_ok, consts_ok = sem("wfr_ok"), sem("wfl_ok"), sem("consts_ok")
        low_sum_ok, low_all, low_flag_ok = sem("low_sum_ok"), sem("low_all"), sem("low_flag_ok")
        half_s_ok, gate_done, up_done = sem("half_s_ok"), sem("gate_done"), sem("up_done")
        tanh_ok, u_ok = sem("tanh_ok"), sem("u_ok")
        h0_ok, h0r_ok, h0l_dve, h0l_pool = sem("h0_ok"), sem("h0r_ok"), sem("h0l_dve"), sem("h0l_pool")
        h1_done, h1r_ok, h1f_ok, h1l_ok = sem("h1_done"), sem("h1r_ok"), sem("h1f_ok"), sem("h1l_ok")
        h2_done, h2r_ok, h2f_ok, h2l_ok = sem("h2_done"), sem("h2r_ok"), sem("h2f_ok"), sem("h2l_ok")
        y_done, yT_ok, yn_done = sem("y_done"), sem("yT_ok"), sem("yn_done")
        z_ok, bn2_ok, mv2_ok, var2_ok, rstd2_ok, out_ok = (
            sem("z_ok"), sem("bn2_ok"), sem("mv2_ok"), sem("var2_ok"), sem("rstd2_ok"), sem("out_ok"))

        block = ctx.enter_context(nc.Block())

        @block.sync
        def _(sp):
            sp.sem_inc(out_stored, 16)
            sp.dma_start(w32[:], wqkv).then_inc(wqkv_in, 16)
            for t in range(NT):
                sp.dma_start(xt32[:, TILE * t:TILE * (t + 1)], xT[:, TILE * t:TILE * (t + 1)]).then_inc(xT_in[t], 16)
                if t == 0:
                    sp.dma_start(vec[:], vecs).then_inc(small_in, 16)
                    sp.dma_start(bvb[:], bv.broadcast_to([P, D])).then_inc(small_in, 16)
            sp.dma_start(ident[:], eye).then_inc(eye_in, 16)
            sp.dma_start(xn[:], x).then_inc(x_in, 16)
            for n in range(WCH):
                if n >= RAW_SLOTS:
                    sp.wait_ge(wfl_ok, n - RAW_SLOTS + 1)
                sp.dma_start(raw[:, n % RAW_SLOTS, :], wffn[:, n, :]).then_inc(raw_in[n % RAW_SLOTS], 16)
            with sp.Fori(0, LAST) as t:
                sp.wait_ge(out_ok, t + 1)
                sp.dma_start(out[:, bass.ts(t, 4), :], z).then_inc(out_stored, 16)
            for a in range(2):
                sp.wait_ge(out_ok, LAST + 1 + a)
                sp.dma_start(out[:, 4 * LAST + 2 * a:4 * LAST + 2 * a + 2, :], z_end[:, 2 * a:2 * a + 2, :]).then_inc(out_stored, 16)
            sp.wait_ge(out_stored, 16 * (NT + 1) + 16)

        @block.tensor
        def _(pe):
            pe.sem_inc(h2_done, 1)
            pe.sem_inc(y_done, 1)
            pe.sem_inc(yn_done, 1)

            def split_product(dst, lhs, rhs, first, last):
                (ar, al), (br, bl) = lhs, rhs
                nc.tensor.matmul(dst, ar, br, start=first, stop=False)
                nc.tensor.matmul(dst, ar, bl, start=False, stop=False)
                return nc.tensor.matmul(dst, al, br, start=False, stop=last)

            def wcol(w):
                return w_r[:, w, :], w_l[:, w, :]

            pe.wait_ge(warm_ok, 1)
            for _ in range(WARM_UPS):
                nc.tensor.matmul(bank[7][:, 0:P], probs[:, 0, 0:P], probs[:, 0, 0:P], start=True, stop=True)

            def project_kq(t):
                cols = slice(TILE * t, TILE * (t + 1))
                pe.wait_ge(xT_l, t + 1)
                split_product(bank[t], wcol(1), (xt_r[:, cols], xt_l[:, cols]), True, True).then_inc(k_done, 1)
                split_product(bank[4 + t], wcol(0), (xt_r[:, cols], xt_l[:, cols]), True, True).then_inc(q_done, 1)

            def project_v(t):
                pe.wait_ge(q32_ok, t + 1)
                for n in range(4):
                    blk = slice(TILE * t + P * n, TILE * t + P * (n + 1))
                    last = split_product(bank[4 + t][:, D * n:D * (n + 1)], (xt_r[:, blk], xt_l[:, blk]), wcol(2), True, True)
                last.then_inc(v_done, 1)

            def scores(s):
                p, b = s // 2, s // 2 % 2
                q = slice(P * (s % 2), P * (s % 2) + P)
                pe.wait_ge(ql_ok, p + 1)
                if s == 0:
                    pe.wait_ge(kl_ok, 2)
                if s == 1:
                    pe.wait_ge(kl_ok, 4)
                if s >= 2:
                    pe.wait_ge(exp_ok, s - 1)
                for h in range(S // TILE):
                    keys = slice(S * b + TILE * h, S * b + TILE * (h + 1))
                    last = split_product(score[s % 2][:, TILE * h:TILE * (h + 1)],
                                         (q_r[:, p % 2, q], q_l[:, p % 2, q]),
                                         (k_r[:, keys], k_l[:, keys]), True, True)
                last.then_inc(s_done, 1)

            def turn_probs(s):
                pe.wait_ge(exp_ok, s + 1)
                for h in range(2):
                    if s == 0:
                        pe.wait_ge(v32_ok, h + 1)
                    else:
                        pe.wait_ge(ptl_ok, 2 * s - 1 + h)
                    for k in range(4):
                        last = nc.tensor.transpose(pt_ps[h][:, P * k:P * (k + 1)],
                                                   probs[:, s % 2, P * (4 * h + k):P * (4 * h + k + 1)], ident[:])
                    last.then_inc(pt_done, 1)

            def weigh_values(p, h):
                b = p % 2
                pe.wait_ge(ptl_ok, 4 * p + 3 + h)
                if h == 0:
                    if p < 2:
                        pe.wait_ge(vl_ok, 2 * p + 2)
                    if p == 0:
                        pe.wait_ge(v32_ok, 3)
                    else:
                        pe.wait_ge(oT_ok, p)
                for k in range(4 * h, 4 * h + 4):
                    last = split_product(pv_ps[:, 0:256], (v_r[:, KB * b + k, :], v_l[:, KB * b + k, :]),
                                         (pt_r[:, p % 2, k, :], pt_l[:, p % 2, k, :]), k == 0, k == KB - 1)
                if h == 1:
                    last.then_inc(pv_done, 1)

            def turn_back(p):
                pe.wait_ge(oT_ok, p + 1)
                if p == 0:
                    pe.wait_ge(v32_ok, 4)
                if p >= 2:
                    pe.wait_ge(x1Tl_ok, p - 1 if p < PAIRS - 1 else p - 2)
                if p:
                    pe.wait_ge(attn_ok, p)
                for u in range(2):
                    last = nc.tensor.transpose(misc_ps[:, D * u:D * (u + 1)], oT[:, p % 2, P * u:P * (u + 1)], ident[:])
                last.then_inc(back_done, 1)

            def turn_x1(p):
                pe.wait_ge(x1_ok, p + 1)
                if x1T_ps[p] is misc_ps:
                    pe.wait_ge(attn_ok, min(p + 2, PAIRS))
                    if p:
                        pe.wait_ge(x1Tl_ok, p if p < PAIRS - 1 else p - 2)
                for u in range(2):
                    last = nc.tensor.transpose(x1T_ps[p][:, P * u:P * (u + 1)], xn[:, 2 * p + u, :], ident[:])
                last.then_inc(x1T_done, 1)

            tile0 = slice(0, TILE)
            pe.wait_ge(wqkv_r, 1)
            pe.wait_ge(xT_r, 1)
            for w, dst in ((1, bank[0]), (0, bank[4])):
                nc.tensor.matmul(dst, w_r[:, w, :], xt_r[:, tile0], start=True, stop=False)
            pe.wait_ge(wqkv_l, 1)
            for w, dst in ((1, bank[0]), (0, bank[4])):
                nc.tensor.matmul(dst, w_l[:, w, :], xt_r[:, tile0], start=False, stop=False)
            pe.wait_ge(xT_l, 1)
            for w, dst, done in ((1, bank[0], k_done), (0, bank[4], q_done)):
                nc.tensor.matmul(dst, w_r[:, w, :], xt_l[:, tile0], start=False, stop=True).then_inc(done, 1)
            project_kq(1)
            project_v(0)
            project_kq(2)
            scores(0)
            project_kq(3)
            project_v(1)
            scores(1)
            pe.wait_ge(eye_in, 16)
            turn_probs(0)
            project_v(2)
            scores(2)
            turn_probs(1)
            project_v(3)
            scores(3)

            def attention_step(s):
                if s < STEPS:
                    turn_probs(s)
                if s + 2 < STEPS:
                    scores(s + 2)
                if s >= 4 and s % 2 == 0:
                    turn_back((s - 4) // 2)
                if s >= 2:
                    weigh_values((s - 2) // 2, s % 2)
                if s >= 7 and s % 2 == 1:
                    turn_x1((s - 7) // 2)

            for s in range(2, STEPS - 3):
                attention_step(s)
            pe.wait_ge(exp_ok, STEPS - 2)
            pe.wait_ge(low_sum_ok, WCH)
            pe.wait_ge(consts_ok, 3)
            nc.tensor.matmul(bank[2][0:1, 0:WCH], ones[:], low_sum[:], start=True, stop=True).then_inc(low_all, 1)
            turn_probs(STEPS - 3)
            pe.wait_ge(low_flag_ok, 1)
            has_low = pe.value_load(low_flag[0:1, 0:1], min_val=0, max_val=2**31 - 1)

            def rest(low):

                def ffn_product(dst, lhs, rhs, first, last):
                    (ar, al), (br, bl) = lhs, rhs
                    nc.tensor.matmul(dst, ar, br, start=first, stop=False)
                    if low:
                        nc.tensor.matmul(dst, al, br, start=False, stop=False)
                    return nc.tensor.matmul(dst, ar, bl, start=False, stop=last)

                def gated(t, c):
                    feats = slice(P * c, P * (c + 1))
                    cols = bass.ts(t, TILE)
                    pe.wait_ge(u_ok, HC * t + c + BUFS)
                    ffn_product(gate_ps, (wf_r[:, W1, feats], wf_l[:, W1, feats]),
                                (xt_r[:, cols], xt_l[:, cols]), True, True).then_inc(gate_done, 1)
                    pe.wait_ge(h0_ok, HC * t + c + 1)
                    ffn_product(up_ps, (wf_r[:, W2, feats], wf_l[:, W2, feats]),
                                (xt_r[:, cols], xt_l[:, cols]), True, True).then_inc(up_done, 1)

                def hidden1(t, c):
                    pe.wait_ge(h1f_ok, HC * t + c + 1)
                    for k in range(HC):
                        if c == 0:
                            pe.wait_ge(h0l_dve if k % 2 else h0l_pool, 2 * t + k // 2 + 2)
                        last = ffn_product(h1_ps[c % 2], (wf_r[:, H1 + k, P * c:P * (c + 1)], wf_l[:, H1 + k, P * c:P * (c + 1)]),
                                           (h0_r[:, k, :], h0_l[:, k, :]), k == 0, k == HC - 1)
                    last.then_inc(h1_done, 1)

                def hidden2(t, c):
                    pe.wait_ge(h2f_ok, HC * t + c + 1)
                    for k in range(HC):
                        if c == 0:
                            pe.wait_ge(h1l_ok, HC * t + k + 1 + BUFS)
                        last = ffn_product(h2_ps[c % 2], (wf_r[:, H2 + k, P * c:P * (c + 1)], wf_l[:, H2 + k, P * c:P * (c + 1)]),
                                           (h1_r[:, k, :], h1_l[:, k, :]), k == 0, k == HC - 1)
                    last.then_inc(h2_done, 1)

                def project(t):
                    pe.wait_ge(yT_ok, t + 1)
                    for k in range(HC):
                        pe.wait_ge(h2l_ok, HC * t + k + 1 + BUFS)
                        last = ffn_product(y_ps, (wf_r[:, W3, P * k:P * (k + 1)], wf_l[:, W3, P * k:P * (k + 1)]),
                                           (h2_r[:, k, :], h2_l[:, k, :]), k == 0, k == HC - 1)
                    last.then_inc(y_done, 1)

                def hidden2_half(a, c):
                    n, half = HC * a + c, slice(HALF * a, HALF * (a + 1))
                    if n < 2:
                        pe.wait_ge(h2f_ok, HC * LAST + n + 1)
                    elif n > 2:
                        pe.wait_ge(h2f_ok, HC * LAST + n - 2 + BUFS)
                    for k in range(HC):
                        if n == 0:
                            pe.wait_ge(h1l_ok, HC * LAST + k + 1 + BUFS)
                        last = ffn_product(h2_end[n % 3][:, 0:HALF], (wf_r[:, H2 + k, P * c:P * (c + 1)], wf_l[:, H2 + k, P * c:P * (c + 1)]),
                                           (h1_r[:, k, half], h1_l[:, k, half]), k == 0, k == HC - 1)
                    last.then_inc(h2_done, 1)

                def project_half(a):
                    half = slice(HALF * a, HALF * (a + 1))
                    if a == 0:
                        pe.wait_ge(yT_ok, LAST + 1)
                    for k in range(HC):
                        pe.wait_ge(h2l_ok, HC * LAST + HC * a + k + 1 + BUFS)
                        last = ffn_product(y_end[a][:, 0:HALF], (wf_r[:, W3, P * k:P * (k + 1)], wf_l[:, W3, P * k:P * (k + 1)]),
                                           (h2_r[:, k, half], h2_l[:, k, half]), k == 0, k == HC - 1)
                    last.then_inc(y_done, 1)

                def turn_y_half(a):
                    pe.wait_ge(yT_ok, LAST + 2 + a)
                    if a == 0:
                        pe.wait_ge(z_ok, LAST + 1)
                    for j in range(2):
                        last = nc.tensor.transpose(yn_end[a][:, D * j:D * (j + 1)], yT[:, HALF * a + P * j:HALF * a + P * (j + 1)], ident[:])
                    last.then_inc(yn_done, 1)

                def turn_y(t):
                    pe.wait_ge(yT_ok, t + 2)
                    pe.wait_ge(z_ok, t + 1)
                    for j in range(4):
                        last = nc.tensor.transpose(yn_ps[:, D * j:D * (j + 1)], yT[:, P * j:P * (j + 1)], ident[:])
                    last.then_inc(yn_done, 1)

                pe.wait_ge(x1Tl_ok, 2)
                scores(STEPS - 1)
                turn_x1(PAIRS - 5)
                weigh_values(PAIRS - 3, 1)
                pe.wait_ge(exp_ok, STEPS - 1)
                gated(0, 0)
                turn_probs(STEPS - 2)
                turn_back(PAIRS - 3)
                weigh_values(PAIRS - 2, 0)
                gated(0, 1)
                turn_probs(STEPS - 1)
                weigh_values(PAIRS - 2, 1)
                gated(0, 2)
                turn_x1(PAIRS - 4)
                weigh_values(PAIRS - 1, 0)
                gated(0, 3)
                turn_back(PAIRS - 2)
                weigh_values(PAIRS - 1, 1)

                gated(1, 0)
                hidden1(0, 0)

                def tile(t, first=False):
                    if first:
                        turn_back(PAIRS - 1)
                    else:
                        gated(t + 1, 0)
                        project(t - 1)
                    hidden1(t, 1)
                    if first:
                        turn_x1(PAIRS - 3)
                    else:
                        turn_y(t - 1)
                    gated(t + 1, 1)
                    if first:
                        turn_x1(PAIRS - 2)
                    hidden1(t, 2)
                    hidden1(t, 3)
                    gated(t + 1, 2)
                    if first:
                        turn_x1(PAIRS - 1)
                        pe.wait_ge(x1Tl_ok, PAIRS - 1)
                    hidden2(t, 0)
                    hidden2(t, 1)
                    gated(t + 1, 3)
                    hidden2(t, 2)
                    hidden2(t, 3)
                    if first:
                        pe.wait_ge(x1Tl_ok, PAIRS)
                    hidden1(t + 1, 0)

                tile(0, first=True)
                with pe.Fori(1, LAST) as t:
                    tile(t)

                for c in range(1, HC):
                    hidden1(LAST, c)
                project(LAST - 1)
                hidden2_half(0, 0)
                turn_y(LAST - 1)
                for c in range(1, HC):
                    hidden2_half(0, c)
                for c in range(HC):
                    hidden2_half(1, c)
                for a in range(2):
                    project_half(a)
                for a in range(2):
                    turn_y_half(a)

            with pe.If(has_low != 0):
                rest(True)
            with pe.Else():
                rest(False)

        @block.scalar
        def _(act):
            for s in (h1f_ok, h2f_ok):
                act.sem_inc(s, BUFS)
            act.sem_inc(yT_ok, 1)

            def round_xT(t):
                act.wait_ge(xT_in[t], 16)
                nc.scalar.copy(xt_r[:, TILE * t:TILE * (t + 1)], xt32[:, TILE * t:TILE * (t + 1)]).then_inc(xT_r, 1)

            def take_k(t):
                cols = slice(TILE * t, TILE * (t + 1))
                act.wait_ge(k_done, t + 1)
                nc.scalar.activation(k_r[:, cols], bank[t], ACT.Identity, bias=vec[:, BK:BK + 1]).then_inc(kr_ok, 1)

            def take_q(t):
                cols = slice(TILE * t, TILE * (t + 1))
                act.wait_ge(q_done, t + 1)
                nc.scalar.activation(q32[:, cols], bank[4 + t], ACT.Identity, bias=bqs[:], scale=SCALE).then_inc(q32_ok, 1)

            def soften(s):
                act.wait_ge(max_ok, s + 1)
                if s >= 2:
                    act.wait_ge(pt_done, 2 * s - 2)
                nc.scalar.activation(probs[:, s % 2, :], score[s % 2], ACT.Exp, bias=negmax[:, s:s + 1],
                                     accum_out=rowsum[:, s:s + 1]).then_inc(exp_ok, 1)

            def round_v(t):
                act.wait_ge(v32_ok, t + 1)
                nc.scalar.copy(v_r[:, 4 * t:4 * t + 4, :], xt32[:, TILE * t:TILE * (t + 1)].rearrange("p (n d) -> p n d", d=D)).then_inc(vr_ok, 1)

            def round_probs(s, h):
                p = s // 2
                act.wait_ge(pt_done, 2 * s + h + 1)
                if p >= 2:
                    act.wait_ge(pv_done, p - 1)
                nc.scalar.copy(pt_r[:, p % 2, 4 * h:4 * h + 4, P * (s % 2):P * (s % 2) + P],
                               pt_ps[h].rearrange("p (k q) -> p k q", q=P)).then_inc(ptr_ok, 1)

            def sum_low(n):
                act.wait_ge(wfl_ok, n + 1)
                if n:
                    act.wait_ge(low_sum_ok, n)
                nc.scalar.activation(low_abs[:], wf_l[:, n, :].bitcast(F32), ACT.Abs, scale=2.0 ** 64,
                                     accum_out=low_sum[:, n:n + 1]).then_inc(low_sum_ok, 1)

            def take_oT(p):
                act.wait_ge(pv_done, p + 1)
                if p >= 2:
                    act.wait_ge(back_done, p - 1)
                nc.scalar.copy(oT[:, p % 2, :], pv_ps[:, 0:256]).then_inc(oT_ok, 1)

            def divide(p):
                act.wait_ge(back_done, p + 1)
                act.wait_ge(rinv_ok, p + 1)
                if p >= 2:
                    act.wait_ge(resid_ok, p - 1)
                for u in range(2):
                    last = nc.scalar.activation(attn[:, p % 2, u, :], misc_ps[:, D * u:D * (u + 1)], ACT.Identity,
                                                scale=rinv[:, 2 * p + u:2 * p + u + 1])
                last.then_inc(attn_ok, 1)

            def round_x1(p):
                act.wait_ge(x1T_done, p + 1)
                nc.scalar.copy(xt_r[:, 256 * p:256 * (p + 1)], x1T_ps[p][:, 0:256]).then_inc(x1Tr_ok, 1)

            def tanh_gate(t, c):
                act.wait_ge(gate_done, HC * t + c + 1)
                act.wait_ge(u_ok, HC * t + c + 1)
                nc.scalar.activation(tanh_g[:, c % 2, :], gate_ps, ACT.Tanh, scale=half_s1[:, c:c + 1]).then_inc(tanh_ok, 1)

            def round_h0(t, c):
                act.wait_ge(h0_ok, HC * t + c + 2)
                nc.scalar.copy(h0_r[:, c, :], h0_32[:, c % 2, :]).then_inc(h0r_ok, 1)

            round_xT(0)
            round_xT(1)
            act.wait_ge(small_in, 32)
            act.wait_ge(bqs_ok, 1)
            take_k(0)
            take_q(0)
            round_xT(2)
            take_k(1)
            take_q(1)
            round_xT(3)
            round_v(0)
            take_k(2)
            take_q(2)
            take_k(3)
            soften(0)
            take_q(3)
            round_v(1)
            for s in range(STEPS + 2):
                if s >= 4 and s % 2 == 0:
                    take_oT((s - 4) // 2)
                if s == STEPS + 1:
                    round_h0(0, 2)
                    tanh_gate(0, 3)
                if s >= 5 and s % 2 == 1:
                    divide((s - 5) // 2)
                if s == STEPS:
                    tanh_gate(0, 2)
                if s >= 8 and s % 2 == 0:
                    round_x1((s - 8) // 2)
                if s == STEPS - 2:
                    act.wait_ge(half_s_ok, 2)
                    tanh_gate(0, 0)
                if s < STEPS:
                    round_probs(s, 0)
                    round_probs(s, 1)
                if s + 1 < STEPS:
                    soften(s + 1)
                if s < 2:
                    round_v(s + 2)
                if 2 <= s < 2 + WCH:
                    sum_low(s - 2)
                if s == STEPS - 2:
                    tanh_gate(0, 1)
                    round_h0(0, 0)
                if s == STEPS:
                    round_h0(0, 1)
            round_h0(0, 3)
            take_oT(PAIRS - 1)
            tanh_gate(1, 0)
            nc.scalar.preload_act_table(ACT.Gelu)

            def gelu(t, c, psum, done, value, scale, dst_r, r_ok, f_ok, l_ok, slot):
                act.wait_ge(done, value)
                nc.scalar.activation(dst_r[:, c, :], psum[c % 2], ACT.Gelu, scale=vec[:, scale + c:scale + c + 1]).then_inc(r_ok, 1)
                act.wait_ge(l_ok, HC * t + c + 1)
                nc.scalar.activation(h32[:, slot + c % 2, :], psum[c % 2], ACT.Gelu, scale=vec[:, scale + c:scale + c + 1]).then_inc(f_ok, 1)

            def gelu1(t, c):
                if c == 0:
                    act.wait_ge(h2_done, HC * t + 1)
                gelu(t, c, h1_ps, h1_done, HC * t + c + 1, HS1, h1_r, h1r_ok, h1f_ok, h1l_ok, 0)

            def gelu2(t, c):
                if c == 0:
                    act.wait_ge(y_done, t + 1)
                gelu(t, c, h2_ps, h2_done, HC * t + c + 2, HS2, h2_r, h2r_ok, h2f_ok, h2l_ok, 2)

            def take_y(t):
                act.wait_ge(y_done, t + 2)
                act.wait_ge(yn_done, t + 1)
                nc.scalar.activation(yT, y_ps, ACT.Identity, scale=vec[:, S3:S3 + 1]).then_inc(yT_ok, 1)

            gelu1(0, 0)

            def gelu2_half(a, c):
                n, half = HC * a + c, slice(HALF * a, HALF * (a + 1))
                act.wait_ge(h2_done, HC * LAST + n + 2)
                if n == 0:
                    act.wait_ge(y_done, LAST + 1)
                nc.scalar.activation(h2_r[:, c, half], h2_end[n % 3][:, 0:HALF], ACT.Gelu, scale=vec[:, HS2 + c:HS2 + c + 1]).then_inc(h2r_ok, 1)
                if n < 2:
                    act.wait_ge(h2l_ok, HC * LAST + n + 1)
                elif n >= 4:
                    act.wait_ge(h2l_ok, HC * LAST + n - 3 + BUFS)
                nc.scalar.activation(h32[:, (n + 2) % 4, 0:HALF], h2_end[n % 3][:, 0:HALF], ACT.Gelu, scale=vec[:, HS2 + c:HS2 + c + 1]).then_inc(h2f_ok, 1)

            def take_y_half(a):
                act.wait_ge(y_done, LAST + 2 + a)
                if a == 0:
                    act.wait_ge(yn_done, LAST + 1)
                nc.scalar.activation(yT[:, HALF * a:HALF * (a + 1)], y_end[a][:, 0:HALF], ACT.Identity, scale=vec[:, S3:S3 + 1]).then_inc(yT_ok, 1)

            def tile(t, first=False):
                if first:
                    divide(PAIRS - 1)
                else:
                    tanh_gate(t + 1, 0)
                    take_y(t - 1)
                gelu1(t, 1)
                if first:
                    round_x1(PAIRS - 3)
                tanh_gate(t + 1, 1)
                if first:
                    round_x1(PAIRS - 2)
                gelu1(t, 2)
                gelu1(t, 3)
                round_h0(t + 1, 0)
                tanh_gate(t + 1, 2)
                round_h0(t + 1, 1)
                if first:
                    round_x1(PAIRS - 1)
                gelu2(t, 0)
                gelu2(t, 1)
                round_h0(t + 1, 2)
                tanh_gate(t + 1, 3)
                gelu2(t, 2)
                round_h0(t + 1, 3)
                gelu2(t, 3)
                gelu1(t + 1, 0)

            tile(0, first=True)
            with act.Fori(1, LAST) as t:
                tile(t)

            for c in range(1, HC):
                gelu1(LAST, c)
            take_y(LAST - 1)
            for a in range(2):
                for c in range(HC):
                    gelu2_half(a, c)
            take_y_half(0)
            take_y_half(1)

        @block.vector
        def _(dve):
            for s in (u_ok, h1l_ok, h2l_ok):
                dve.sem_inc(s, BUFS)
            for s in (h0_ok, h0l_dve, z_ok):
                dve.sem_inc(s, 1)

            dve.wait_ge(wqkv_in, 16)
            nc.vector.tensor_copy(w_r, w32[:]).then_inc(wqkv_r, 1)
            dve.wait_ge(wqkv_r, 1)
            nc.vector.tensor_tensor(w_l, w32[:], w_r.bitcast(F32), ALU.subtract).then_inc(wqkv_l, 1)

            def split_xT(t):
                cols = slice(TILE * t, TILE * (t + 1))
                dve.wait_ge(xT_r, t + 1)
                nc.vector.tensor_tensor(xt_l[:, cols], xt32[:, cols], xt_r[:, cols].bitcast(F32), ALU.subtract).then_inc(xT_l, 1)

            def split_k(t):
                cols = slice(TILE * t, TILE * (t + 1))
                dve.wait_ge(kr_ok, t + 1)
                nc.vector.scalar_tensor_tensor(out=k_l[:, cols], in0=bank[t], scalar=vec[:, BK:BK + 1],
                                               in1=k_r[:, cols].bitcast(F32), op0=ALU.add, op1=ALU.subtract).then_inc(kl_ok, 1)

            split_xT(0)
            dve.wait_ge(small_in, 32)
            nc.vector.tensor_scalar(bqs[:], vec[:, BQ:BQ + 1], SCALE, None, ALU.mult).then_inc(bqs_ok, 1)
            nc.vector.tensor_scalar(half_s1[:], vec[:, S1:S1 + HC], 0.5, None, ALU.mult).then_inc(half_s_ok, 1)
            dve.wait_ge(half_s_ok, 1)
            nc.vector.tensor_tensor(half_s1s2[:], half_s1[:], vec[:, S2:S2 + HC], ALU.mult).then_inc(half_s_ok, 1)

            def row_max(s):
                dve.wait_ge(s_done, s + 1)
                nc.vector.tensor_reduce(negmax[:, s:s + 1], score[s % 2], AX.X, ALU.max, negate=True).then_inc(max_ok, 1)

            def bias_v(t):
                dve.wait_ge(v_done, t + 1)
                dst = xt32[:, TILE * t:TILE * (t + 1)].rearrange("p (n d) -> p n d", d=D)
                src = bank[4 + t].rearrange("p (n d) -> p n d", d=D)
                nc.vector.tensor_tensor(dst, src, bvb[:].unsqueeze(1).broadcast_to([P, 4, D]), ALU.add).then_inc(v32_ok, 1)

            def split_probs(s, h):
                p = s // 2
                dve.wait_ge(ptr_ok, 2 * s + h + 1)
                q = slice(P * (s % 2), P * (s % 2) + P)
                nc.vector.tensor_tensor(pt_l[:, p % 2, 4 * h:4 * h + 4, q], pt_ps[h].rearrange("p (k q) -> p k q", q=P),
                                        pt_r[:, p % 2, 4 * h:4 * h + 4, q].bitcast(F32), ALU.subtract).then_inc(ptl_ok, 1)

            def invert_sums(p):
                dve.wait_ge(exp_ok, 2 * p + 2)
                nc.vector.reciprocal(rinv[:, 2 * p:2 * p + 2], rowsum[:, 2 * p:2 * p + 2]).then_inc(rinv_ok, 1)

            def stats1(p):
                dve.wait_ge(resid_ok, p + 1)
                if p:
                    dve.wait_ge(mv1_ok, p)
                for u in range(2):
                    nc.vector.bn_stats(bn6[:, u, :], xn[:, 2 * p + u, :]).then_inc(bn1_ok, 1)
                for u in range(2):
                    dve.wait_ge(bn1_ok, 2 * p + u + 1)
                    last = nc.vector.bn_aggr(mv1[:, 2 * p + u, :], bn6[:, u, :])
                last.then_inc(mv1_ok, 1)

            def normalise1(p):
                dve.wait_ge(rstd1_ok, p + 1)
                for s in (2 * p, 2 * p + 1):
                    last = nc.vector.tensor_scalar(xn[:, s, :], xn[:, s, :], mv1[:, s, 0:1], rstd1[:, s:s + 1], ALU.subtract, ALU.mult)
                last.then_inc(x1_ok, 1)

            def split_x1(p):
                dve.wait_ge(x1Tr_ok, p + 1)
                nc.vector.tensor_tensor(xt_l[:, 256 * p:256 * (p + 1)], x1T_ps[p][:, 0:256],
                                        xt_r[:, 256 * p:256 * (p + 1)].bitcast(F32), ALU.subtract).then_inc(x1Tl_ok, 1)

            def round_weights(n):
                dve.wait_ge(raw_in[n % RAW_SLOTS], 16 * (n // RAW_SLOTS + 1))
                nc.vector.tensor_copy(wf_r[:, n, :], raw[:, n % RAW_SLOTS, :]).then_inc(wfr_ok, 1)

            def gate_u(t, c):
                dve.wait_ge(tanh_ok, HC * t + c + 1)
                nc.vector.scalar_tensor_tensor(out=u32[:, c % 2, :], in0=tanh_g[:, c % 2, :], scalar=1.0,
                                               in1=gate_ps, op0=ALU.add, op1=ALU.mult).then_inc(u_ok, 1)

            def gate_h0(t, c):
                dve.wait_ge(u_ok, HC * t + c + 1 + BUFS)
                dve.wait_ge(up_done, HC * t + c + 1)
                dve.wait_ge(h0l_dve if c % 2 else h0l_pool, 2 * t + c // 2 + 1)
                nc.vector.scalar_tensor_tensor(out=h0_32[:, c % 2, :], in0=up_ps, scalar=half_s1s2[:, c:c + 1],
                                               in1=u32[:, c % 2, :], op0=ALU.mult, op1=ALU.mult).then_inc(h0_ok, 1)

            def gate(t, c):
                gate_u(t, c)
                gate_h0(t, c)

            def split_h0(t, c):
                dve.wait_ge(h0r_ok, HC * t + c + 1)
                nc.vector.tensor_tensor(h0_l[:, c, :], h0_32[:, c % 2, :], h0_r[:, c, :].bitcast(F32), ALU.subtract).then_inc(h0l_dve, 1)

            split_xT(1)
            split_k(0)
            split_xT(2)
            split_k(1)
            bias_v(0)
            split_xT(3)
            split_k(2)
            row_max(0)
            split_k(3)
            bias_v(1)
            row_max(1)
            for s in range(STEPS + 2):
                if s == STEPS:
                    gate(0, 2)
                if s >= 8 and s % 2 == 0:
                    split_x1((s - 8) // 2)
                if s == STEPS - 2:
                    dve.wait_ge(half_s_ok, 2)
                    gate(0, 0)
                if s == STEPS - 3:
                    dve.wait_ge(low_all, 1)
                    nc.vector.tensor_reduce(low_flag[:].bitcast(F32), bank[2][0:1, 0:WCH], AX.X, ALU.add).then_inc(low_flag_ok, 1)
                if s < STEPS:
                    split_probs(s, 0)
                    split_probs(s, 1)
                if s < 2:
                    bias_v(s + 2)
                if s + 2 < STEPS:
                    row_max(s + 2)
                if s % 2 == 1 and s < STEPS:
                    invert_sums(s // 2)
                if s >= 6 and s % 2 == 0 and s < STEPS:
                    stats1((s - 6) // 2)
                if s < WCH:
                    round_weights(s)
                if s == STEPS - 2:
                    gate(0, 1)
                if s == STEPS:
                    split_h0(0, 1)
                if s == STEPS + 1:
                    gate(0, 3)
                    stats1(PAIRS - 3)
                    split_h0(0, 3)
                    stats1(PAIRS - 2)
            gate(1, 0)
            normalise1(PAIRS - 2)

            def split_h(t, c, f_ok, slot, dst_r, dst_l, l_ok):
                dve.wait_ge(f_ok, HC * t + c + 1 + BUFS)
                nc.vector.tensor_tensor(dst_l[:, c, :], h32[:, slot + c % 2, :], dst_r[:, c, :].bitcast(F32), ALU.subtract).then_inc(l_ok, 1)

            def split_h1(t, c):
                split_h(t, c, h1f_ok, 0, h1_r, h1_l, h1l_ok)

            def split_h2(t, c):
                split_h(t, c, h2f_ok, 2, h2_r, h2_l, h2l_ok)

            def add_residual2(t):
                dve.wait_ge(yn_done, t + 2)
                dve.wait_ge(out_stored, 16 * t + 16)
                nc.vector.tensor_tensor(z, yn_ps.rearrange("p (j d) -> p j d", d=D),
                                        xn[:, bass.ts(t, 4), :], ALU.add).then_inc(z_ok, 1)

            def stats2(t):
                dve.wait_ge(z_ok, t + 2)
                for j in range(4):
                    last = nc.vector.bn_stats(bn6[:, j, :], z[:, j, :])
                dve.drain()
                for j in range(4):
                    last = nc.vector.bn_aggr(mv2[:, j, :], bn6[:, j, :])
                last.then_inc(mv2_ok, 1)

            def normalise2(t):
                dve.wait_ge(rstd2_ok, t + 1)
                for j in range(4):
                    last = nc.vector.tensor_scalar(z[:, j, :], z[:, j, :], mv2[:, j, 0:1], rstd2[:, j:j + 1], ALU.subtract, ALU.mult)
                last.then_inc(out_ok, 1)

            split_h1(0, 0)

            def tile(t, first=False):
                if first:
                    stats1(PAIRS - 1)
                else:
                    gate(t + 1, 0)
                    add_residual2(t - 1)
                split_h1(t, 1)
                if first:
                    split_x1(PAIRS - 3)
                gate(t + 1, 1)
                if first:
                    normalise1(PAIRS - 1)
                    split_x1(PAIRS - 2)
                else:
                    stats2(t - 1)
                split_h1(t, 2)
                split_h1(t, 3)
                gate_u(t + 1, 2)
                split_h0(t + 1, 1)
                gate_h0(t + 1, 2)
                if first:
                    split_x1(PAIRS - 1)
                else:
                    normalise2(t - 1)
                split_h2(t, 0)
                split_h2(t, 1)
                gate(t + 1, 3)
                split_h2(t, 2)
                split_h0(t + 1, 3)
                split_h2(t, 3)
                split_h1(t + 1, 0)

            tile(0, first=True)
            with dve.Fori(1, LAST) as t:
                tile(t)

            def split_h2_half(a, c):
                n, half = HC * a + c, slice(HALF * a, HALF * (a + 1))
                dve.wait_ge(h2f_ok, HC * LAST + n + 1 + BUFS)
                nc.vector.tensor_tensor(h2_l[:, c, half], h32[:, (n + 2) % 4, 0:HALF], h2_r[:, c, half].bitcast(F32), ALU.subtract).then_inc(h2l_ok, 1)

            def add_residual2_half(a):
                two = slice(2 * a, 2 * a + 2)
                dve.wait_ge(yn_done, LAST + 2 + a)
                nc.vector.tensor_tensor(z_end[:, two, :], yn_end[a][:, 0:HALF].rearrange("p (j d) -> p j d", d=D),
                                        xn[:, 4 * LAST + 2 * a:4 * LAST + 2 * a + 2, :], ALU.add).then_inc(z_ok, 1)

            def stats2_half(a):
                dve.wait_ge(z_ok, LAST + 2 + a)
                for j in (2 * a, 2 * a + 1):
                    nc.vector.bn_stats(bn6[:, j, :], z_end[:, j, :])
                dve.drain()
                for j in (2 * a, 2 * a + 1):
                    last = nc.vector.bn_aggr(mv2[:, j, :], bn6[:, j, :])
                last.then_inc(mv2_ok, 1)

            def normalise2_half(a):
                dve.wait_ge(rstd2_ok, LAST + 1 + a)
                for j in (2 * a, 2 * a + 1):
                    last = nc.vector.tensor_scalar(z_end[:, j, :], z_end[:, j, :], mv2[:, j, 0:1], rstd2[:, j:j + 1], ALU.subtract, ALU.mult)
                last.then_inc(out_ok, 1)

            for c in range(1, HC):
                split_h1(LAST, c)
            split_h2_half(0, 0)
            add_residual2(LAST - 1)
            split_h2_half(0, 1)
            stats2(LAST - 1)
            split_h2_half(0, 2)
            split_h2_half(0, 3)
            normalise2(LAST - 1)
            split_h2_half(1, 0)
            split_h2_half(1, 1)
            split_h2_half(1, 2)
            split_h2_half(1, 3)
            add_residual2_half(0)
            stats2_half(0)
            add_residual2_half(1)
            stats2_half(1)
            normalise2_half(0)
            normalise2_half(1)

        @block.gpsimd
        def _(pool):
            pool.sem_inc(h0l_pool, 1)
            nc.gpsimd.memset(probs[:, 0, 0:P], 0.0).then_inc(warm_ok, 1)
            nc.gpsimd.memset(mhalf[:], -0.5).then_inc(consts_ok, 1)
            nc.gpsimd.memset(eps[:], EPS).then_inc(consts_ok, 1)
            nc.gpsimd.memset(ones[:], 1.0).then_inc(consts_ok, 1)

            def split_q(p):
                i, b = p // 2, p % 2
                src = q32[:, S * b + 256 * i:S * b + 256 * (i + 1)]
                if p < 4:
                    pool.wait_ge(q32_ok, 2 * b + i // 2 + 1)
                if p >= 2:
                    pool.wait_ge(s_done, 2 * p - 2)
                nc.gpsimd.tensor_copy(q_r[:, p % 2, :], src).then_inc(qr_ok, 1)
                pool.wait_ge(qr_ok, p + 1)
                nc.gpsimd.tensor_tensor(q_l[:, p % 2, :], src, q_r[:, p % 2, :].bitcast(F32), ALU.subtract).then_inc(ql_ok, 1)

            def split_v(t):
                pool.wait_ge(vr_ok, t + 1)
                src = xt32[:, TILE * t:TILE * (t + 1)].rearrange("p (n d) -> p n d", d=D)
                nc.gpsimd.tensor_tensor(v_l[:, 4 * t:4 * t + 4, :], src, v_r[:, 4 * t:4 * t + 4, :].bitcast(F32), ALU.subtract).then_inc(vl_ok, 1)

            def add_residual(p):
                pool.wait_ge(attn_ok, p + 1)
                if p == 0:
                    pool.wait_ge(x_in, 16)
                nc.gpsimd.tensor_tensor(xn[:, 2 * p:2 * p + 2, :], attn[:, p % 2, :, :], xn[:, 2 * p:2 * p + 2, :], ALU.add).then_inc(resid_ok, 1)

            def normalise1(p):
                two = slice(2 * p, 2 * p + 2)
                pool.wait_ge(mv1_ok, p + 1)
                nc.gpsimd.tensor_scalar(rstd1[:, two], mv1[:, two, 1], EPS, None, ALU.add).then_inc(var1_ok, 1)
                pool.wait_ge(var1_ok, p + 1)
                pool.wait_ge(consts_ok, 3)
                nc.gpsimd.tensor_tensor(rstd1[:, two], rstd1[:, two], mhalf[:, 0:2], ALU.pow).then_inc(rstd1_ok, 1)
                if p < PAIRS - 2:
                    nc.gpsimd.tensor_tensor(xn[:, two, :], xn[:, two, :], mv1[:, two, 0:1].broadcast_to([P, 2, D]), ALU.subtract).then_inc(centre1_ok, 1)
                    pool.wait_ge(rstd1_ok, p + 1)
                    pool.wait_ge(centre1_ok, p + 1)
                    nc.gpsimd.tensor_tensor(xn[:, two, :], xn[:, two, :], rstd1[:, two].unsqueeze(2).broadcast_to([P, 2, D]), ALU.mult).then_inc(x1_ok, 1)

            def split_weights(n):
                pool.wait_ge(wfr_ok, n + 1)
                nc.gpsimd.tensor_tensor(wf_l[:, n, :], raw[:, n % RAW_SLOTS, :], wf_r[:, n, :].bitcast(F32), ALU.subtract).then_inc(wfl_ok, 1)

            def split_h0(t, c):
                pool.wait_ge(h0r_ok, HC * t + c + 1)
                nc.gpsimd.tensor_tensor(h0_l[:, c, :], h0_32[:, c % 2, :], h0_r[:, c, :].bitcast(F32), ALU.subtract).then_inc(h0l_pool, 1)

            split_q(0)
            split_v(0)
            split_q(1)
            split_v(1)
            for s in range(STEPS + 2):
                if s % 2 == 0 and s // 2 + 2 < PAIRS:
                    split_q(s // 2 + 2)
                if s >= 5 and s % 2 == 1 and s < STEPS:
                    add_residual((s - 5) // 2)
                if s == STEPS:
                    split_h0(0, 2)
                    add_residual(PAIRS - 2)
                if s >= 6 and s % 2 == 0:
                    normalise1((s - 6) // 2)
                if s < 2:
                    split_v(s + 2)
                if s < WCH:
                    split_weights(s)
                if s == STEPS - 2:
                    split_h0(0, 0)
            normalise1(PAIRS - 2)
            add_residual(PAIRS - 1)
            normalise1(PAIRS - 1)

            def invert_std2(t, rows=slice(0, 4)):
                pool.wait_ge(mv2_ok, t + 1)
                nc.gpsimd.tensor_tensor(rstd2[:, rows], mv2[:, rows, 1], eps[:, rows], ALU.add).then_inc(var2_ok, 1)
                pool.wait_ge(var2_ok, t + 1)
                nc.gpsimd.tensor_tensor(rstd2[:, rows], rstd2[:, rows], mhalf[:, rows], ALU.pow).then_inc(rstd2_ok, 1)

            def tile(t, first=False):
                if not first:
                    invert_std2(t - 1)
                split_h0(t + 1, 0)
                split_h0(t + 1, 2)

            tile(0, first=True)
            with pool.Fori(1, LAST) as t:
                tile(t)

            invert_std2(LAST - 1)
            for a in range(2):
                invert_std2(LAST + a, slice(2 * a, 2 * a + 2))


def kernel(L0_attn_X, L0_attn_W_q, L0_attn_W_k, L0_attn_W_v, L0_attn_b_q, L0_attn_b_k, L0_attn_b_v,
           L0_ffn_w1_w, L0_ffn_w1_s, L0_ffn_w2_w, L0_ffn_w2_s, L0_ffn_h1_w, L0_ffn_h1_s,
           L0_ffn_h2_w, L0_ffn_h2_s, L0_ffn_w3_w, L0_ffn_w3_s):
    import numpy as np
    import concourse.bacc as bacc
    from concourse.bass_utils import run_bass_kernel_spmd

    def chunked(w):
        wt = np.asarray(w).T
        return wt.reshape(-1, P, wt.shape[1]).transpose(1, 0, 2)

    def column(v):
        return np.asarray(v).reshape(-1, P).T

    x = np.ascontiguousarray(L0_attn_X)
    arrays = {
        "x": np.ascontiguousarray(x.reshape(B, NT, 2, P, D).transpose(3, 1, 0, 2, 4)).reshape(P, STEPS, D),
        "xT": np.ascontiguousarray(x.reshape(B * S, D).T),
        "wqkv": np.ascontiguousarray(np.stack([L0_attn_W_q, L0_attn_W_k, L0_attn_W_v], axis=1)),
        "bv": np.ascontiguousarray(L0_attn_b_v).reshape(1, D),
        "vecs": np.ascontiguousarray(np.concatenate([column(v) for v in (
            L0_attn_b_q, L0_attn_b_k, L0_ffn_w1_s, L0_ffn_w2_s, L0_ffn_h1_s, L0_ffn_h2_s, L0_ffn_w3_s)], axis=1)),
        "wffn": np.ascontiguousarray(np.concatenate(
            [chunked(L0_ffn_w1_w), chunked(L0_ffn_w2_w), chunked(L0_ffn_w3_w).reshape(P, 1, HID),
             chunked(L0_ffn_h1_w), chunked(L0_ffn_h2_w)], axis=1)),
        "eye": np.eye(P, dtype=np.float32),
    }
    nc = bacc.Bacc("TRN2", target_bir_lowering=False, num_devices=1)
    args = [nc.dram_tensor(n, arrays[n].shape, mybir.dt.from_np(arrays[n].dtype), kind="ExternalInput").ap()
            for n in ("xT", "x", "wqkv", "bv", "vecs", "wffn", "eye")]
    args.append(nc.dram_tensor("out", (P, STEPS, D), F32, kind="ExternalOutput").ap())
    build(nc, *args)
    r = run_bass_kernel_spmd(nc, [arrays], core_ids=[0])
    by_step = r.results[0]["out"].reshape(P, NT, B, 2, D)
    return np.ascontiguousarray(by_step.transpose(2, 1, 3, 0, 4)).reshape(B, S, D)
```
